# Optimizing a Trainium2 kernel written in Bass

```python
import numpy as np
import jax
import jax.numpy as jnp

def _softmax(x, axis=-1):
    return jax.nn.softmax(x, axis=axis)

def _gelu(x):
    return jax.nn.gelu(x, approximate=True)

def _silu(x):
    return jax.nn.silu(x)

def _sigmoid(x):
    return jax.nn.sigmoid(x)

def _layernorm(x, axis=-1, eps=1e-05):
    m = jnp.mean(x, axis=axis, keepdims=True)
    v = jnp.var(x, axis=axis, keepdims=True)
    return (x - m) / jnp.sqrt(v + eps)

def _scatter_add(tgt, idx, src, axis=0):
    return tgt.at[idx].add(src)

def _segment_sum(src, seg, n):
    return jax.ops.segment_sum(src, seg, n)
kernel_name = 'mk_cond_seq_d2_seqx_r8_2ebdb4'

def setup_inputs(seed: int=0):
    np.random.seed(seed)
    _w = jnp.asarray

    def _rec_inputs():
        import jax
        import jax.numpy as jnp
        _rk = jax.random.key(seed)
        x = 1.648e-05 + 1 * jax.random.normal(jax.random.fold_in(_rk, 1), (8, 128, 144), jnp.float32)
        _lenS = 128 - jax.random.randint(jax.random.fold_in(_rk, 7), (8,), 0, max(1, 128 // 4) + 1, jnp.int32)
        _lenS2 = 128 - jax.random.randint(jax.random.fold_in(_rk, 8), (8,), 0, max(1, 128 // 4) + 1, jnp.int32)
        cond_1152 = 0.00914911 + 1.00357 * jax.random.normal(jax.random.fold_in(_rk, 11), (8, 144), jnp.float32)
        return (x, cond_1152)
    x, cond_1152 = _rec_inputs()

    def _L0_cond_setup():
        import jax, jax.numpy as jnp
        import numpy as np
        B, L, C = (8, 128, 144)
        H = 16
        D = C // H
        FF = int(C * 4.0)
        EPS = 1e-06

        def _layernorm(x):
            mu = jnp.mean(x, axis=-1, keepdims=True)
            var = jnp.mean(jnp.square(x - mu), axis=-1, keepdims=True)
            return (x - mu) * jax.lax.rsqrt(var + EPS)

        def _modulate(x, shift, scale):
            return x * (1.0 + scale) + shift

        def _attention(h, W_qkv, b_qkv, W_proj, b_proj):
            b, l, c = h.shape
            qkv = h @ W_qkv + b_qkv
            qkv = qkv.reshape(b, l, 3, H, D)
            q, k, v = (qkv[:, :, 0], qkv[:, :, 1], qkv[:, :, 2])
            scale = D ** (-0.5)
            scores = jnp.einsum('blhd,bmhd->bhlm', q * scale, k)
            attn = jax.nn.softmax(scores, axis=-1)
            o = jnp.einsum('bhlm,bmhd->blhd', attn, v).reshape(b, l, c)
            return o @ W_proj + b_proj
        key = jax.random.key(seed)
        ks = jax.random.split(key, 12)
        s = 0.02
        return {'x': jax.random.normal(ks[0], (B, L, C), jnp.float32), 'c': jax.random.normal(ks[1], (B, 1, C), jnp.float32), 'W_qkv': jax.random.normal(ks[2], (C, 3 * C), jnp.float32) * s, 'b_qkv': jnp.zeros((3 * C,), jnp.float32), 'W_proj': jax.random.normal(ks[3], (C, C), jnp.float32) * s, 'b_proj': jnp.zeros((C,), jnp.float32), 'W_fc1': jax.random.normal(ks[4], (C, FF), jnp.float32) * s, 'b_fc1': jnp.zeros((FF,), jnp.float32), 'W_fc2': jax.random.normal(ks[5], (FF, C), jnp.float32) * s, 'b_fc2': jnp.zeros((C,), jnp.float32), 'W_ada': jax.random.normal(ks[6], (C, 6 * C), jnp.float32) * s, 'b_ada': jnp.zeros((6 * C,), jnp.float32)}
    _L0_cond_all = _L0_cond_setup()
    _L0_cond_in = {k: v for k, v in _L0_cond_all.items() if k in ('W_qkv', 'b_qkv', 'W_proj', 'b_proj', 'W_fc1', 'b_fc1', 'W_fc2', 'b_fc2', 'W_ada', 'b_ada')}
    del _L0_cond_all

    def _L1_cond_setup():
        import math
        import jax, jax.numpy as jnp
        import numpy as np
        B, T, D = (8, 128, 144)
        H = 16
        E = 4
        EPS = 1e-06

        def _layer_norm(x):
            mu = jnp.mean(x, axis=-1, keepdims=True)
            var = jnp.mean(jnp.square(x - mu), axis=-1, keepdims=True)
            return (x - mu) * jax.lax.rsqrt(var + EPS)

        def _modulate(x, shift, scale):
            return x * (1.0 + scale) + shift

        def _attention(y, qkv_w, qkv_b, out_w, out_b):
            b, t, d = y.shape
            hd = d // H
            qkv = y @ qkv_w + qkv_b
            q, k, v = jnp.split(qkv, 3, axis=-1)
            q = q.reshape(b, t, H, hd).transpose(0, 2, 1, 3)
            k = k.reshape(b, t, H, hd).transpose(0, 2, 1, 3)
            v = v.reshape(b, t, H, hd).transpose(0, 2, 1, 3)
            scores = jnp.einsum('bhqd,bhkd->bhqk', q, k) / math.sqrt(hd)
            attn = jax.nn.softmax(scores, axis=-1)
            out = jnp.einsum('bhqk,bhkd->bhqd', attn, v)
            out = out.transpose(0, 2, 1, 3).reshape(b, t, d)
            return out @ out_w + out_b
        key = jax.random.key(seed)
        ks = jax.random.split(key, 12)
        std = 0.02
        return {'x': jax.random.normal(ks[0], (B, T, D), dtype=jnp.float32), 'c': jax.random.normal(ks[1], (B, D), dtype=jnp.float32), 'qkv_w': jax.random.normal(ks[2], (D, 3 * D), dtype=jnp.float32) * std, 'qkv_b': jnp.zeros((3 * D,), dtype=jnp.float32), 'out_w': jax.random.normal(ks[3], (D, D), dtype=jnp.float32) * std, 'out_b': jnp.zeros((D,), dtype=jnp.float32), 'w1': jax.random.normal(ks[4], (D, E * D), dtype=jnp.float32) * std, 'b1': jnp.zeros((E * D,), dtype=jnp.float32), 'w2': jax.random.normal(ks[5], (E * D, D), dtype=jnp.float32) * std, 'b2': jnp.zeros((D,), dtype=jnp.float32), 'ada_w': jax.random.normal(ks[6], (D, 6 * D), dtype=jnp.float32) * std, 'ada_b': jnp.zeros((6 * D,), dtype=jnp.float32)}
    _L1_cond_all = _L1_cond_setup()
    _L1_cond_in = {k: v for k, v in _L1_cond_all.items() if k in ('qkv_w', 'qkv_b', 'out_w', 'out_b', 'w1', 'b1', 'w2', 'b2', 'ada_w', 'ada_b')}
    del _L1_cond_all
    return {'x': x, 'cond_1152': cond_1152, 'L0_cond_W_qkv': _L0_cond_in['W_qkv'], 'L0_cond_b_qkv': _L0_cond_in['b_qkv'], 'L0_cond_W_proj': _L0_cond_in['W_proj'], 'L0_cond_b_proj': _L0_cond_in['b_proj'], 'L0_cond_W_fc1': _L0_cond_in['W_fc1'], 'L0_cond_b_fc1': _L0_cond_in['b_fc1'], 'L0_cond_W_fc2': _L0_cond_in['W_fc2'], 'L0_cond_b_fc2': _L0_cond_in['b_fc2'], 'L0_cond_W_ada': _L0_cond_in['W_ada'], 'L0_cond_b_ada': _L0_cond_in['b_ada'], 'L1_cond_qkv_w': _L1_cond_in['qkv_w'], 'L1_cond_qkv_b': _L1_cond_in['qkv_b'], 'L1_cond_out_w': _L1_cond_in['out_w'], 'L1_cond_out_b': _L1_cond_in['out_b'], 'L1_cond_w1': _L1_cond_in['w1'], 'L1_cond_b1': _L1_cond_in['b1'], 'L1_cond_w2': _L1_cond_in['w2'], 'L1_cond_b2': _L1_cond_in['b2'], 'L1_cond_ada_w': _L1_cond_in['ada_w'], 'L1_cond_ada_b': _L1_cond_in['ada_b']}

def reference(x, cond_1152, L0_cond_W_qkv, L0_cond_b_qkv, L0_cond_W_proj, L0_cond_b_proj, L0_cond_W_fc1, L0_cond_b_fc1, L0_cond_W_fc2, L0_cond_b_fc2, L0_cond_W_ada, L0_cond_b_ada, L1_cond_qkv_w, L1_cond_qkv_b, L1_cond_out_w, L1_cond_out_b, L1_cond_w1, L1_cond_b1, L1_cond_w2, L1_cond_b2, L1_cond_ada_w, L1_cond_ada_b):
    import jax
    import jax.numpy as jnp

    def _L0_cond_ref(x, c, W_qkv, b_qkv, W_proj, b_proj, W_fc1, b_fc1, W_fc2, b_fc2, W_ada, b_ada):
        import jax, jax.numpy as jnp
        import numpy as np
        B, L, C = (8, 128, 144)
        H = 16
        D = C // H
        FF = int(C * 4.0)
        EPS = 1e-06

        def _layernorm(x):
            mu = jnp.mean(x, axis=-1, keepdims=True)
            var = jnp.mean(jnp.square(x - mu), axis=-1, keepdims=True)
            return (x - mu) * jax.lax.rsqrt(var + EPS)

        def _modulate(x, shift, scale):
            return x * (1.0 + scale) + shift

        def _attention(h, W_qkv, b_qkv, W_proj, b_proj):
            b, l, c = h.shape
            qkv = h @ W_qkv + b_qkv
            qkv = qkv.reshape(b, l, 3, H, D)
            q, k, v = (qkv[:, :, 0], qkv[:, :, 1], qkv[:, :, 2])
            scale = D ** (-0.5)
            scores = jnp.einsum('blhd,bmhd->bhlm', q * scale, k)
            attn = jax.nn.softmax(scores, axis=-1)
            o = jnp.einsum('bhlm,bmhd->blhd', attn, v).reshape(b, l, c)
            return o @ W_proj + b_proj
        ada = jax.nn.silu(c) @ W_ada + b_ada
        shift_msa, scale_msa, gate_msa, shift_mlp, scale_mlp, gate_mlp = jnp.split(ada, 6, axis=-1)
        h = _modulate(_layernorm(x), shift_msa, scale_msa)
        x = x + gate_msa * _attention(h, W_qkv, b_qkv, W_proj, b_proj)
        h = _modulate(_layernorm(x), shift_mlp, scale_mlp)
        mlp = jax.nn.gelu(h @ W_fc1 + b_fc1, approximate=True) @ W_fc2 + b_fc2
        x = x + gate_mlp * mlp
        return x

    def _L1_cond_ref(x, c, qkv_w, qkv_b, out_w, out_b, w1, b1, w2, b2, ada_w, ada_b):
        import math
        import jax, jax.numpy as jnp
        import numpy as np
        B, T, D = (8, 128, 144)
        H = 16
        E = 4
        EPS = 1e-06

        def _layer_norm(x):
            mu = jnp.mean(x, axis=-1, keepdims=True)
            var = jnp.mean(jnp.square(x - mu), axis=-1, keepdims=True)
            return (x - mu) * jax.lax.rsqrt(var + EPS)

        def _modulate(x, shift, scale):
            return x * (1.0 + scale) + shift

        def _attention(y, qkv_w, qkv_b, out_w, out_b):
            b, t, d = y.shape
            hd = d // H
            qkv = y @ qkv_w + qkv_b
            q, k, v = jnp.split(qkv, 3, axis=-1)
            q = q.reshape(b, t, H, hd).transpose(0, 2, 1, 3)
            k = k.reshape(b, t, H, hd).transpose(0, 2, 1, 3)
            v = v.reshape(b, t, H, hd).transpose(0, 2, 1, 3)
            scores = jnp.einsum('bhqd,bhkd->bhqk', q, k) / math.sqrt(hd)
            attn = jax.nn.softmax(scores, axis=-1)
            out = jnp.einsum('bhqk,bhkd->bhqd', attn, v)
            out = out.transpose(0, 2, 1, 3).reshape(b, t, d)
            return out @ out_w + out_b
        mods = (jax.nn.silu(c) @ ada_w + ada_b)[:, None, :]
        m0, m1, m2, m3, m4, m5 = jnp.split(mods, 6, axis=-1)
        y = _modulate(_layer_norm(x), m0, m1)
        x = x + m2 * _attention(y, qkv_w, qkv_b, out_w, out_b)
        y = _modulate(_layer_norm(x), m3, m4)
        y = jax.nn.gelu(y @ w1 + b1, approximate=True)
        x = x + m5 * (y @ w2 + b2)
        return x
    x = _L0_cond_ref(x, cond_1152[:, None, :], L0_cond_W_qkv, L0_cond_b_qkv, L0_cond_W_proj, L0_cond_b_proj, L0_cond_W_fc1, L0_cond_b_fc1, L0_cond_W_fc2, L0_cond_b_fc2, L0_cond_W_ada, L0_cond_b_ada)
    x = _L1_cond_ref(x, cond_1152, L1_cond_qkv_w, L1_cond_qkv_b, L1_cond_out_w, L1_cond_out_b, L1_cond_w1, L1_cond_b1, L1_cond_w2, L1_cond_b2, L1_cond_ada_w, L1_cond_ada_b)
    return x

_drawn_inputs = setup_inputs


def setup_inputs(seed=0):
    import zlib

    import numpy as np

    out = dict(_drawn_inputs(seed))
    spreads = {'L0_cond_b_qkv': (0.0, 0.8),
     'L0_cond_b_proj': (0.0, 0.502),
     'L0_cond_b_fc1': (0.0, 0.8),
     'L0_cond_b_fc2': (0.0, 0.49),
     'L0_cond_b_ada': (0.0, 0.502),
     'L1_cond_qkv_b': (0.0, 0.8),
     'L1_cond_out_b': (0.0, 0.465),
     'L1_cond_b1': (0.0, 0.8),
     'L1_cond_b2': (0.0, 0.455),
     'L1_cond_ada_b': (0.0, 0.55)}
    factors = {'L0_cond_W_qkv': 8.0,
     'L0_cond_W_proj': 8.0,
     'L0_cond_W_fc1': 5.304,
     'L0_cond_W_fc2': 4.926,
     'L0_cond_W_ada': 2.722,
     'L1_cond_qkv_w': 8.0,
     'L1_cond_out_w': 8.0,
     'L1_cond_w1': 5.313,
     'L1_cond_w2': 4.839}
    for name, (base, spread) in spreads.items():
        noise = np.random.default_rng([zlib.crc32(name.encode()), seed]).standard_normal(out[name].shape)
        drawn = base * np.exp(spread * noise) if base else spread * noise
        out[name] = jnp.asarray(drawn.astype(out[name].dtype))
    for name, factor in factors.items():
        out[name] = (out[name] * factor).astype(out[name].dtype)
    return out
```

```python
import concourse.bass as bass
from concourse import mybir
from contextlib import ExitStack


def dit_two_blocks(nc, x, cond_t, w_ada, b_ada, w_qkv, b_qkv, w_proj, b_proj, w_fc1, b_fc1, w_fc2, b_fc2,
                   identity, row_marks, out):
    F32 = mybir.dt.float32
    F32R = mybir.dt.float32r
    ALU = mybir.AluOpType
    ACT = mybir.ActivationFunctionType
    AX = mybir.AxisListType

    B, T, C = x.shape
    L = w_qkv.shape[0]
    P = 128
    H = 16
    D = C // H
    R = C - P
    F = w_fc1.shape[2]
    MT = -(-F // P)
    FR = F - (MT - 1) * P
    HP = P // 4
    G = H // 4
    GB = 4
    NG = B // GB
    BANK = 512
    HALF = H * T // 2
    EPS = 1e-6
    SCALE = 1.0 / 3.0
    ADA = 6 * C
    SHIFT1, SCALE1, GATE1, SHIFT2, SCALE2, GATE2 = (k * C for k in range(6))
    LO_R, HI_R, ONES, LO_A = C, C + R, C + 2 * R, 2 * P
    MAX_HI, MAX_LO = 3 * D, 3 * D + 1

    ctx = ExitStack()
    with ctx:
        def sb(name, shape, dt=F32):
            return ctx.enter_context(nc.sbuf_tensor(name, shape, dt))

        def sem(name):
            return ctx.enter_context(nc.semaphore(name))

        X = sb("X", [P, B, C])
        MODS = sb("MODS", [P, B, ADA])
        ident = sb("ident", [P, P])
        ident_r = sb("ident_r", [P, P], F32R)
        consts = sb("consts", [P, 2])
        lowm, bias_row = consts[:, 0:1], consts[:, 1:2]
        cT = sb("cT", [P, 2, B])
        ce = sb("ce", [P, 2, B])
        cr = sb("cr", [P, 2, B])
        cs = sb("cs", [P, 2, B])
        wada = sb("wada", [P, 2, ADA])
        ada = sb("ada", [B, L, ADA])
        raw_q = sb("raw_q", [P, 2, 3 * C])
        wq = sb("wq", [P, 3, 3 * C], F32R)
        raw_1 = sb("raw_1", [P, 2, MT * P])
        w1 = sb("w1", [P, 3, MT * P], F32R)
        split_hi = sb("split_hi", [P, MT * P], F32R)
        split_lo = sb("split_lo", [P, MT * P])
        w2 = sb("w2", [P, MT, C])
        wp = sb("wp", [P, 2, C])
        bst = sb("bst", [P, 2, 6])
        mv = sb("mv", [P, 2, 2])
        veps = sb("veps", [P, 2])
        rstd = sb("rstd", [P, 2])
        mhalf = sb("mhalf", [P, 1])
        h1 = sb("h1", [P, C])
        hf = sb("hf", [P, 2, C])
        HS = sb("HS", [P, 2, 3 * P], F32R)
        HT = sb("HT", [P, 3, T], F32R)
        HTM = sb("HTM", [P, NG, 3, GB * T], F32R)
        QK = sb("QK", [P, 2, 2, H * HP], F32R)
        V = sb("V", [P, 3, H * HP])
        KT = sb("KT", [P, 2, G * T], F32R)
        Q1T = sb("Q1T", [P, G * T], F32R)
        Q2T = sb("Q2T", [P, G * T], F32R)
        KBD = sb("KBD", [P, G, 4 * T], F32R)
        QBD = sb("QBD", [P, G, 4 * T], F32R)
        nm = sb("nm", [P, H])
        Pr = sb("Pr", [P, H * T])
        OT = sb("OT", [P, G * T])
        rs = sb("rs", [P, H])
        o = sb("o", [P, 2 * P])
        oT = sb("oT", [P, 2, T])
        tmp = sb("tmp", [P, 2, C])
        GE = sb("GE", [P, NG, MT, GB * T])

        S1 = ctx.enter_context(nc.psum_tensor("S1", [P, 2 * BANK], F32))
        S2 = ctx.enter_context(nc.psum_tensor("S2", [P, 2 * BANK], F32))
        b4, b5, b6, b7 = (ctx.enter_context(nc.psum_tensor(f"bank{i}", [P, BANK], F32)) for i in (4, 5, 6, 7))
        fc1_bank = [S1[:, 0:BANK], S1[:, BANK:], S2[:, 0:BANK], S2[:, BANK:]]
        ada_dram = nc.dram_tensor("ada_scratch", (L, B, ADA), F32, kind="Internal").ap()

        x_in = [sem("x_first_in"), sem("x_rest_in")]
        const_in = sem("const_in")
        cond_in = sem("cond_in")
        wada_in = sem("wada_in")
        raw_q_in = sem("raw_q_in")
        raw_1_in = sem("raw_1_in")
        w2_in = sem("w2_in")
        wp_in = sem("wp_in")
        mods_in = [sem(f"mods_in{b}") for b in range(B)]
        kbd_in = sem("kbd_in")
        qbd_in = sem("qbd_in")
        out_done = sem("out_done")
        ada_out = sem("ada_out")
        dve_step = sem("dve_step")
        pool_step = sem("pool_step")
        zeroed = sem("zeroed")
        cleared = sem("cleared")
        zeroed_pool = sem("zeroed_pool")
        silu_e = sem("silu_e")
        silu_done = sem("silu_done")
        ada_mm = sem("ada_mm")
        ada_ready = sem("ada_ready")
        wq_ready = sem("wq_ready")
        w1_ready = sem("w1_ready")
        stats_done = sem("stats_done")
        rstd_done = sem("rstd_done")
        h_ready = sem("h_ready")
        hs_hi = sem("hs_hi")
        hs_lo = sem("hs_lo")
        t1_done = sem("t1_done")
        ht_evac = sem("ht_evac")
        qkv_done = sem("qkv_done")
        split_done = sem("split_done")
        lo_done = sem("lo_done")
        tk_done = sem("tk_done")
        tq_done = sem("tq_done")
        kt_evac = sem("kt_evac")
        q1_evac = sem("q1_evac")
        s1_done = [sem("s1a_done"), sem("s1b_done")]
        max_done = [sem("maxa_done"), sem("maxb_done")]
        nm_done = sem("nm_done")
        t3_done = sem("t3_done")
        q2_evac = sem("q2_evac")
        s2_done = [sem("s2a_done"), sem("s2b_done")]
        exp_done = [sem("expa_done"), sem("expb_done")]
        pv_done = [sem("pva_done"), sem("pvb_done")]
        ot_evac = sem("ot_evac")
        t4_done = sem("t4_done")
        norm_done = sem("norm_done")
        t5_done = sem("t5_done")
        o_evac = sem("o_evac")
        proj_done = sem("proj_done")
        mul_done = sem("mul_done")
        x1_done = sem("x1_done")
        fc1_done = sem("fc1_done")
        gelu_done = sem("gelu_done")
        fc2_done = sem("fc2_done")
        mul2_done = sem("mul2_done")
        x2_done = sem("x2_done")

        def heads(ap):
            return ap.rearrange("p (h r) -> p h r", r=HP)

        block = ctx.enter_context(nc.Block())

        @block.sync
        def _(sp):
            def load(to, frm, s):
                sp.dma_start(to, frm).then_inc(s, 16)

            sp.wait_ge(cleared, 1)
            load(cT[:, 0, :], cond_t[0:P, :], cond_in)
            load(cT[0:R, 1, :], cond_t[P:C, :], cond_in)

            def load_ada(l):
                load(wada[:, 0, :], w_ada[l, 0:P, :], wada_in)
                load(wada[0:R, 1, :], w_ada[l, P:C, :], wada_in)
                load(wada[R:R + 1, 1, :], b_ada[l:l + 1, :], wada_in)

            sp.wait_ge(cleared, 2)
            load_ada(0)
            load(X[:, 0, :], x[0, :, :], x_in[0])
            load(ident[:], identity, const_in)
            load(consts[:], row_marks, const_in)

            def load_raw(raw, w, b, l, n, s):
                load(raw[:, 0, 0:n], w[l, 0:P, :], s)
                for k in range(3):
                    load(raw[k * R:(k + 1) * R, 1, 0:n], w[l, P:C, :], s)
                for k in (3 * R, 3 * R + 1):
                    load(raw[k:k + 1, 1, 0:n], b[l:l + 1, :], s)

            def load_layer(l):
                if l > 0:
                    sp.wait_ge(wq_ready, l)
                load_raw(raw_q, w_qkv, b_qkv, l, 3 * C, raw_q_in)
                if l > 0:
                    sp.wait_ge(proj_done, B * l)
                load(wp[:, 0, :], w_proj[l, 0:P, :], wp_in)
                load(wp[0:R, 1, :], w_proj[l, P:C, :], wp_in)
                load(wp[R:R + 1, 1, :], b_proj[l:l + 1, :], wp_in)

            def load_mlp(l):
                if l > 0:
                    sp.wait_ge(w1_ready, l)
                load_raw(raw_1, w_fc1, b_fc1, l, F, raw_1_in)
                if l > 0:
                    sp.wait_ge(fc2_done, B * l)
                for m in range(MT - 1):
                    load(w2[:, m, :], w_fc2[l, m * P:(m + 1) * P, :], w2_in)
                load(w2[0:FR, MT - 1, :], w_fc2[l, (MT - 1) * P:F, :], w2_in)
                load(w2[FR:FR + 1, MT - 1, :], b_fc2[l:l + 1, :], w2_in)

            def load_mods(l):
                for b in range(B):
                    if l > 0:
                        sp.wait_ge(mul2_done, B * (l - 1) + b + 1)
                    load(MODS[:, b, :], ada_dram[l, b:b + 1, :].broadcast_to([P, ADA]), mods_in[b])

            sp.wait_ge(cleared, 4)
            sp.wait_ge(zeroed_pool, 1)
            load_layer(0)
            load(X[:, 1:B, :], x[1:B, :, :].rearrange("b t c -> t b c"), x_in[1])
            sp.wait_ge(ada_mm, 1)
            load_ada(1)
            for l in range(L):
                sp.wait_ge(ada_ready, l + 1)
                load(ada_dram[l, :, :], ada[:, l, :], ada_out)
                if l == 0:
                    sp.wait_ge(ada_out, 16)
                    load_mods(0)
            sp.wait_ge(ada_out, 16 * L)
            load_mlp(0)

            def move_k(n, par):
                sp.wait_ge(kt_evac, n + 1)
                if n > 0:
                    sp.wait_ge(s1_done[1], n)
                for j in range(4):
                    r = slice(HP * j, HP * j + MAX_HI)
                    load(KBD[r, :, j * T:(j + 1) * T].bitcast(F32),
                         KT[r, par, :].rearrange("p (g t) -> p g t", g=G).bitcast(F32), kbd_in)

            def move_q(n):
                sp.wait_ge(q2_evac, n + 1)
                if n > 0:
                    sp.wait_ge(s2_done[1], n)
                for j in range(4):
                    r = slice(HP * j, HP * (j + 1))
                    load(QBD[r, :, j * T:(j + 1) * T].bitcast(F32),
                         Q2T[r, :].rearrange("p (g t) -> p g t", g=G).bitcast(F32), qbd_in)

            for l in range(L):
                for i in range(-1, B):
                    if i + 1 < B:
                        move_k(B * l + i + 1, (i + 1) % 2)
                    if i >= 0:
                        move_q(B * l + i)
                if l + 1 < L:
                    load_layer(l + 1)
                    load_mods(l + 1)
                    load_mlp(l + 1)
            for b in range(B):
                sp.wait_ge(x2_done, B * (L - 1) + b + 1)
                load(out[b, :, :], X[:, b, :], out_done)
            sp.wait_ge(out_done, 16 * B)

        @block.gpsimd
        def _(pool):
            steps = [0]

            def link(ins):
                steps[0] += 1
                ins.then_inc(pool_step, 1)
                pool.wait_ge(pool_step, steps[0])

            nc.gpsimd.memset(mhalf[:], -0.5)
            nc.gpsimd.memset(w2[:], 0.0)
            nc.gpsimd.memset(wp[:], 0.0)
            nc.gpsimd.memset(GE[:, :, MT - 1, :], 1.0)
            nc.gpsimd.memset(V[:], 0.0).then_inc(zeroed_pool, 1)

            def split_weights(raw, w, n, ready):
                nc.gpsimd.tensor_copy(w[:, 0, 0:n], raw[:, 0, 0:n])
                link(nc.gpsimd.tensor_copy(split_hi[:, 0:n], raw[:, 1, 0:n]))
                nc.gpsimd.tensor_tensor(w[:, 1, 0:n], raw[:, 0, 0:n], w[:, 0, 0:n].bitcast(F32), ALU.subtract)
                link(nc.gpsimd.tensor_scalar(split_lo[:, 0:n], split_hi[:, 0:n].bitcast(F32), lowm, 1.0,
                                             ALU.mult, ALU.mult))
                nc.gpsimd.tensor_tensor(w[:, 2, 0:n], raw[:, 1, 0:n], split_lo[:, 0:n],
                                        ALU.subtract).then_inc(ready, 1)

            def inv_std(q):
                pool.wait_ge(stats_done, q + 1)
                link(nc.gpsimd.tensor_scalar(veps[:, q % 2:q % 2 + 1], mv[:, q % 2, 1:2], 1.0, EPS, ALU.mult, ALU.add))
                nc.gpsimd.tensor_tensor(rstd[:, q % 2:q % 2 + 1], veps[:, q % 2:q % 2 + 1], mhalf[:],
                                        ALU.pow).then_inc(rstd_done, 1)

            def low_part(q):
                hs, h = HS[:, q % 2, :], hf[:, q % 2, :]
                pool.wait_ge(hs_hi, q + 1)
                nc.gpsimd.tensor_tensor(hs[:, LO_A:LO_A + P], h[:, 0:P], hs[:, 0:P].bitcast(F32), ALU.subtract)
                nc.gpsimd.tensor_tensor(hs[:, LO_R:LO_R + R], h[:, P:C], hs[:, P:C].bitcast(F32), ALU.subtract)
                nc.gpsimd.tensor_copy(hs[:, HI_R:HI_R + R], hs[:, P:C].bitcast(F32)).then_inc(hs_lo, 1)

            pool.wait_ge(const_in, 32)
            for l in range(L):
                q0 = 2 * B * l
                pool.wait_ge(raw_q_in, 96 * (l + 1))
                if l > 0:
                    pool.wait_ge(qkv_done, B * l)
                split_weights(raw_q, wq, 3 * C, wq_ready)
                for b in range(2 * B):
                    inv_std(q0 + b)
                    low_part(q0 + b)
                    if b == 3:
                        pool.wait_ge(raw_1_in, 96 * (l + 1))
                        if l > 0:
                            pool.wait_ge(fc1_done, MT * NG * l)
                        split_weights(raw_1, w1, MT * P, w1_ready)

        @block.scalar
        def _(act):
            act.wait_ge(cond_in, 32)
            nc.scalar.activation(ce[:], cT[:], ACT.Exp, scale=-1.0).then_inc(silu_e, 1)
            act.wait_ge(zeroed, 1)
            act.wait_ge(zeroed_pool, 1)

            def high_part(q):
                act.wait_ge(h_ready, q + 1)
                if q >= 2:
                    act.wait_ge(t1_done, q - 1)
                nc.scalar.copy(HS[:, q % 2, 0:C], hf[:, q % 2, :]).then_inc(hs_hi, 1)

            def evac_ht(q, n):
                act.wait_ge(t1_done, q + 1)
                if n > 0:
                    act.wait_ge(qkv_done, n)
                nc.scalar.copy(HT[:].rearrange("p k t -> p (k t)"), b4[:, 0:3 * T]).then_inc(ht_evac, 1)

            def split_qkv(n):
                par = n % 2
                act.wait_ge(qkv_done, n + 1)
                if n >= 2:
                    act.wait_ge(t3_done, n - 1)
                if n >= 3:
                    act.wait_ge(pv_done[1], n - 2)
                for k, slot in ((0, 0), (1, D)):
                    src = b5[:, k * C:(k + 1) * C].rearrange("p (h d) -> p h d", d=D)
                    dst = heads(QK[:, par, k, :])[:, :, slot:slot + 2 * D].rearrange("p h (s d) -> p h s d", d=D)
                    nc.scalar.copy(dst, src.unsqueeze(2).broadcast_to([P, H, 2, D]))
                nc.scalar.copy(heads(V[:, n % 3, :])[:, :, 0:D],
                               b5[:, 2 * C:3 * C].rearrange("p (h d) -> p h d", d=D)).then_inc(split_done, 1)

            def evac_q1(n):
                act.wait_ge(tq_done, n + 1)
                if n > 0:
                    act.wait_ge(s1_done[1], n)
                nc.scalar.copy(Q1T[:], b7[:]).then_inc(q1_evac, 1)

            def evac_q2(n):
                act.wait_ge(t3_done, n + 1)
                if n > 0:
                    act.wait_ge(qbd_in, 64 * n)
                nc.scalar.copy(Q2T[:], b6[:]).then_inc(q2_evac, 1)

            def exp_half(n, half):
                act.wait_ge(s2_done[half], n + 1)
                if n > 0:
                    act.wait_ge(pv_done[half], n)
                nc.scalar.activation(Pr[:, half * HALF:(half + 1) * HALF], S2[:], ACT.Exp,
                                     scale=SCALE).then_inc(exp_done[half], 1)

            def evac_ot(n):
                act.wait_ge(pv_done[1], n + 1)
                if n > 0:
                    act.wait_ge(t4_done, n)
                nc.scalar.copy(OT[:], b7[:]).then_inc(ot_evac, 1)

            def evac_o(n):
                act.wait_ge(t5_done, n + 1)
                if n > 0:
                    act.wait_ge(proj_done, n)
                nc.scalar.copy(oT[:].rearrange("p k t -> p (k t)"), b4[:, 0:2 * T]).then_inc(o_evac, 1)

            def evac_htm(q, n, g):
                bank = (b4, b7)[n % 2]
                act.wait_ge(t1_done, q + 1)
                gg = n // GB
                if gg >= NG:
                    act.wait_ge(fc1_done, MT * (gg - 1))
                c = (n % GB) * T
                nc.scalar.copy(HTM[:, g, :, c:c + T],
                               bank[:, 0:3 * T].rearrange("p (k t) -> p k t", k=3)).then_inc(ht_evac, 1)

            def gelu(gg, g, m):
                act.wait_ge(fc1_done, MT * gg + m + 1)
                if gg >= NG:
                    act.wait_ge(fc2_done, GB * (gg - 1))
                rows = P if m < MT - 1 else FR
                nc.scalar.activation(GE[0:rows, g, m, :], fc1_bank[(MT * gg + m) % 4][0:rows, :],
                                     ACT.Gelu_apprx_tanh).then_inc(gelu_done, 1)

            for l in range(L):
                q0, n0 = 2 * B * l, B * l
                for i in range(-2, B + 2):
                    if 0 <= i + 1 < B:
                        evac_ht(q0 + i + 1, n0 + i + 1)
                        split_qkv(n0 + i + 1)
                    if 0 <= i - 1 < B:
                        exp_half(n0 + i - 1, 0)
                    if 0 <= i + 1 < B:
                        evac_q1(n0 + i + 1)
                    if 0 <= i - 1 < B:
                        exp_half(n0 + i - 1, 1)
                    if 0 <= i - 2 < B:
                        evac_o(n0 + i - 2)
                    if 0 <= i < B:
                        evac_q2(n0 + i)
                    if 0 <= i - 1 < B:
                        evac_ot(n0 + i - 1)
                    if i + 2 < B:
                        high_part(q0 + i + 2)
                qm = q0 + B
                high_part(qm)
                for b in range(GB):
                    high_part(qm + b + 1)
                    evac_htm(qm + b, n0 + b, 0)
                for m in range(MT):
                    gelu(NG * l, 0, m)
                    if m < GB:
                        if GB + m + 1 < B:
                            high_part(qm + GB + m + 1)
                        evac_htm(qm + GB + m, n0 + GB + m, 1)
                for m in range(MT):
                    gelu(NG * l + 1, 1, m)

        @block.vector
        def _(dve):
            steps = [0]

            def link(ins):
                steps[0] += 1
                ins.then_inc(dve_step, 1)
                dve.wait_ge(dve_step, steps[0])

            nc.vector.memset(cT[:], 0.0).then_inc(cleared, 1)
            nc.vector.memset(wada[:, 1, :], 0.0).then_inc(cleared, 1)
            nc.vector.memset(raw_q[:, 1, :], 0.0).then_inc(cleared, 1)
            nc.vector.memset(raw_1[:], 0.0).then_inc(cleared, 1)
            dve.wait_ge(cond_in, 32)
            dve.wait_ge(silu_e, 1)
            link(nc.vector.tensor_scalar_add(ce[:], ce[:], 1.0))
            link(nc.vector.reciprocal(cr[:], ce[:]))
            link(nc.vector.tensor_tensor(cs[:], cT[:], cr[:], ALU.mult))
            dve.wait_ge(const_in, 32)
            nc.vector.tensor_scalar_add(cs[:, 1, :], cs[:, 1, :], bias_row)
            nc.vector.tensor_copy(ident_r[:], ident[:]).then_inc(silu_done, 1)
            nc.vector.memset(KBD[:].bitcast(F32), 0.0)
            nc.vector.memset(QBD[:].bitcast(F32), 0.0)
            nc.vector.memset(QK[:].bitcast(F32), 0.0)
            link(nc.vector.memset(HS[:].bitcast(F32), 0.0))
            nc.vector.memset(HS[:, :, ONES:ONES + 2].bitcast(F32), 1.0)
            for par in range(2):
                nc.vector.memset(heads(QK[:, par, 1, :])[:, :, MAX_HI:MAX_LO + 1].bitcast(F32), 1.0)
            link(nc.vector.memset(o[:], 0.0))
            nc.vector.memset(o[:, C:C + 1], 1.0)
            dve.wait_ge(zeroed_pool, 1)
            nc.vector.memset(V[:].rearrange("p a (h r) -> p (a h) r", r=HP)[:, :, D:D + 1], 1.0).then_inc(zeroed, 1)
            for l in range(L):
                dve.wait_ge(ada_mm, l + 1)
                for k in range(2):
                    bank = (b4, b5)[k] if l == 0 else (b6, b7)[k]
                    link(nc.vector.tensor_copy(ada[:, l, 3 * C * k:3 * C * (k + 1)], bank[0:B, 0:3 * C]))
                v = ada[:, l, :].rearrange("b (k c) -> b k c", k=2)[:, :, C:2 * C]
                nc.vector.tensor_scalar_add(v, v, 1.0).then_inc(ada_ready, 1)

            def norm_stats(q, b):
                link(nc.vector.bn_stats(bst[:, q % 2, :], X[:, b, :]))
                nc.vector.bn_aggr(mv[:, q % 2, :], bst[:, q % 2, :]).then_inc(stats_done, 1)

            def modulate(q, b, scale, shift):
                dve.wait_ge(stats_done, q + 1)
                link(nc.vector.scalar_tensor_tensor(out=h1[:], in0=X[:, b, :], scalar=mv[:, q % 2, 0:1],
                                                    in1=MODS[:, b, scale:scale + C],
                                                    op0=ALU.subtract, op1=ALU.mult))
                dve.wait_ge(rstd_done, q + 1)
                if q >= 2:
                    dve.wait_ge(hs_lo, q - 1)
                nc.vector.scalar_tensor_tensor(out=hf[:, q % 2, :], in0=h1[:], scalar=rstd[:, q % 2:q % 2 + 1],
                                               in1=MODS[:, b, shift:shift + C],
                                               op0=ALU.mult, op1=ALU.add).then_inc(h_ready, 1)

            def low_qk(n):
                par = n % 2
                dve.wait_ge(split_done, n + 1)
                for k, slot in ((0, 2 * D), (1, 0)):
                    v = heads(QK[:, par, k, :])
                    last = nc.vector.tensor_tensor(v[:, :, slot:slot + D],
                                                   b5[:, k * C:(k + 1) * C].rearrange("p (h d) -> p h d", d=D),
                                                   v[:, :, D:2 * D].bitcast(F32), ALU.subtract)
                last.then_inc(lo_done, 1)

            def evac_kt(n):
                dve.wait_ge(tk_done, n + 1)
                if n >= 2:
                    dve.wait_ge(s2_done[1], n - 1)
                nc.vector.tensor_copy(KT[:, n % 2, :], b6[:]).then_inc(kt_evac, 1)

            def neg_max(n, half):
                dve.wait_ge(s1_done[half], n + 1)
                nc.vector.tensor_reduce(nm[:, half * H // 2:(half + 1) * H // 2],
                                        S1[:].rearrange("p (h t) -> p h t", t=T), AX.X, ALU.max,
                                        negate=True).then_inc(max_done[half], 1)

            def split_max(n):
                v = heads(QK[:, n % 2, 0, :])
                m = nm[:].unsqueeze(2)
                dve.wait_ge(max_done[1], n + 1)
                link(nc.vector.tensor_copy(v[:, :, MAX_HI:MAX_HI + 1], m))
                nc.vector.tensor_tensor(v[:, :, MAX_LO:MAX_LO + 1], m, v[:, :, MAX_HI:MAX_HI + 1].bitcast(F32),
                                        ALU.subtract).then_inc(nm_done, 1)

            def normalise(n):
                v = heads(b5[:])
                dve.wait_ge(t4_done, n + 1)
                link(nc.vector.reciprocal(rs[:].unsqueeze(2), v[:, :, D:D + 1]))
                if n > 0:
                    dve.wait_ge(t5_done, n)
                nc.vector.tensor_tensor(o[:, 0:C].rearrange("p (h d) -> p h d", d=D), v[:, :, 0:D],
                                        rs[:].unsqueeze(2).broadcast_to([P, H, D]), ALU.mult).then_inc(norm_done, 1)

            def residual(n, b, product, done, gate, mul, ready):
                dve.wait_ge(done, n + 1)
                nc.vector.tensor_tensor(tmp[:, n % 2, :], product, MODS[:, b, gate:gate + C], ALU.mult).then_inc(mul, 1)
                dve.wait_ge(mul, n + 1)
                nc.vector.tensor_tensor(X[:, b, :], X[:, b, :], tmp[:, n % 2, :], ALU.add).then_inc(ready, 1)

            for l in range(L):
                q0, n0 = 2 * B * l, B * l
                for i in range(-2, B + 2):
                    if 0 <= i < B:
                        neg_max(n0 + i, 0)
                    if 0 <= i + 1 < B:
                        low_qk(n0 + i + 1)
                    if 0 <= i < B:
                        neg_max(n0 + i, 1)
                        split_max(n0 + i)
                    if 0 <= i + 1 < B:
                        evac_kt(n0 + i + 1)
                    if i + 2 < B:
                        b = i + 2
                        if l == 0:
                            if b < 2:
                                dve.wait_ge(x_in[b], 16)
                            dve.wait_ge(mods_in[b], 16)
                        else:
                            dve.wait_ge(mods_in[b], 16 * (l + 1))
                            dve.wait_ge(x2_done, n0 - B + b + 1)
                        norm_stats(q0 + b, b)
                    if 0 <= i - 2 < B:
                        residual(n0 + i - 2, i - 2, b4[:, 2 * T:2 * T + C], proj_done, GATE1, mul_done, x1_done)
                    if i + 2 < B:
                        modulate(q0 + i + 2, i + 2, SCALE1, SHIFT1)
                    if 0 <= i - 1 < B:
                        normalise(n0 + i - 1)
                qm = q0 + B
                for b in range(B):
                    dve.wait_ge(x1_done, n0 + b + 1)
                    norm_stats(qm + b, b)
                    modulate(qm + b, b, SCALE2, SHIFT2)
                for b in range(B):
                    n = n0 + b
                    residual(n, b, (b5, b6)[n % 2][:, 0:C], fc2_done, GATE2, mul2_done, x2_done)

        @block.tensor
        def _(pe):
            pe.wait_ge(silu_done, 1)
            for l in range(L):
                pe.wait_ge(wada_in, 48 * (l + 1))
                for k in range(2):
                    bank = (b4, b5)[k] if l == 0 else (b6, b7)[k]
                    cols = slice(3 * C * k, 3 * C * (k + 1))
                    nc.tensor.matmul(bank[0:B, 0:3 * C], cs[:, 0, :], wada[:, 0, cols], start=True, stop=False)
                    last = nc.tensor.matmul(bank[0:B, 0:3 * C], cs[:, 1, :], wada[:, 1, cols], start=False, stop=True)
                last.then_inc(ada_mm, 1)
            pe.wait_ge(zeroed, 1)
            pe.wait_ge(ada_ready, 2)

            def transpose_h(q, bank):
                pe.wait_ge(hs_lo, q + 1)
                for k in range(3):
                    last = nc.tensor.transpose(bank[:, k * T:(k + 1) * T].bitcast(F32R),
                                               HS[:, q % 2, k * P:(k + 1) * P], ident_r[:])
                last.then_inc(t1_done, 1)

            def qkv(l, b, q, n):
                if b == 0:
                    pe.wait_ge(wq_ready, l + 1)
                    if l > 0:
                        pe.wait_ge(mul2_done, B * l)
                elif b >= 3:
                    pe.wait_ge(norm_done, n - 2)
                pe.wait_ge(ht_evac, q + 1)
                if n > 0:
                    pe.wait_ge(lo_done, n)
                pairs = ((0, 0), (0, 1), (1, 2), (2, 0))
                for k, (h, w) in enumerate(pairs):
                    last = nc.tensor.matmul(b5[:, 0:3 * C], HT[:, h, :], wq[:, w, :], start=(k == 0), stop=(k == 3))
                last.then_inc(qkv_done, 1)

            def transpose_qk(b, n):
                pe.wait_ge(lo_done, n + 1)
                if b >= 2:
                    pe.wait_ge(q2_evac, n - 1)
                if b == 1:
                    pe.wait_ge(kt_evac, n)
                for g in range(G):
                    last = nc.tensor.transpose(b6[:, g * T:(g + 1) * T].bitcast(F32R),
                                               QK[:, n % 2, 1, g * P:(g + 1) * P], ident_r[:])
                last.then_inc(tk_done, 1)
                if b >= 3:
                    pe.wait_ge(ot_evac, n - 2)
                for g in range(G):
                    last = nc.tensor.transpose(b7[:, g * T:(g + 1) * T].bitcast(F32R),
                                               QK[:, n % 2, 0, g * P:(g + 1) * P], ident_r[:])
                last.then_inc(tq_done, 1)

            def scores_for_max(n, half):
                if half == 0:
                    pe.wait_ge(kbd_in, 64 * (n + 1))
                    pe.wait_ge(q1_evac, n + 1)
                    if n > 0:
                        pe.wait_ge(max_done[1], n)
                else:
                    pe.wait_ge(max_done[0], n + 1)
                for k in range(2):
                    g = 2 * half + k
                    last = nc.tensor.matmul(S1[:, k * BANK:(k + 1) * BANK], Q1T[:, g * T:(g + 1) * T], KBD[:, g, :],
                                            start=True, stop=True)
                last.then_inc(s1_done[half], 1)

            def transpose_q2(b, n):
                pe.wait_ge(nm_done, n + 1)
                pe.wait_ge(kt_evac, n + 2 if b + 1 < B else n + 1)
                for g in range(G):
                    last = nc.tensor.transpose(b6[:, g * T:(g + 1) * T].bitcast(F32R),
                                               QK[:, n % 2, 0, g * P:(g + 1) * P], ident_r[:])
                last.then_inc(t3_done, 1)

            def scores_less_max(n, half):
                if half == 0:
                    pe.wait_ge(qbd_in, 64 * (n + 1))
                    if n > 0:
                        pe.wait_ge(exp_done[1], n)
                else:
                    pe.wait_ge(exp_done[0], n + 1)
                for k in range(2):
                    g = 2 * half + k
                    last = nc.tensor.matmul(S2[:, k * BANK:(k + 1) * BANK], KT[:, n % 2, g * T:(g + 1) * T],
                                            QBD[:, g, :], start=True, stop=True)
                last.then_inc(s2_done[half], 1)

            def values(b, n, half):
                pe.wait_ge(exp_done[half], n + 1)
                if half == 0:
                    if b + 2 < B:
                        pe.wait_ge(q1_evac, n + 3)
                    elif n > 0:
                        pe.wait_ge(ot_evac, n)
                for h in range(half * H // 2, (half + 1) * H // 2):
                    g, j = h // 4, h % 4
                    last = nc.tensor.matmul(b7[HP * j:HP * (j + 1), g * T:(g + 1) * T],
                                            V[:, n % 3, HP * h:HP * (h + 1)], Pr[:, h * T:(h + 1) * T],
                                            start=True, stop=True)
                last.then_inc(pv_done[half], 1)

            def transpose_ot(b, n):
                pe.wait_ge(ot_evac, n + 1)
                if b + 2 < B:
                    pe.wait_ge(lo_done, n + 3)
                elif n > 0:
                    pe.wait_ge(norm_done, n)
                for g in range(G):
                    last = nc.tensor.transpose(b5[:, g * T:(g + 1) * T], OT[:, g * T:(g + 1) * T], ident[:])
                last.then_inc(t4_done, 1)

            def transpose_o(n):
                pe.wait_ge(norm_done, n + 1)
                if n > 0:
                    pe.wait_ge(mul_done, n)
                for k in range(2):
                    last = nc.tensor.transpose(b4[:, k * T:(k + 1) * T], o[:, k * P:(k + 1) * P], ident[:])
                last.then_inc(t5_done, 1)

            def project(l, n):
                pe.wait_ge(o_evac, n + 1)
                pe.wait_ge(wp_in, 48 * (l + 1))
                for k in range(2):
                    last = nc.tensor.matmul(b4[:, 2 * T:2 * T + C], oT[:, k, :], wp[:, k, :], start=(k == 0), stop=(k == 1))
                last.then_inc(proj_done, 1)

            def transpose_hm(l, b, q, n):
                if b == 0:
                    pe.wait_ge(mul_done, n + B)
                elif b == 1:
                    pe.wait_ge(ot_evac, B * (l + 1))
                else:
                    pe.wait_ge(ht_evac, q - 1)
                transpose_h(q, (b4, b7)[n % 2])

            def fc1(l, g, m):
                gg = NG * l + g
                k = MT * gg + m
                if m == 0:
                    pe.wait_ge(ht_evac, 2 * B * l + B + GB * (g + 1))
                    pe.wait_ge(w1_ready, l + 1)
                if k >= 4:
                    pe.wait_ge(gelu_done, k - 3)
                pairs = ((0, 0), (0, 2), (1, 0), (2, 1))
                for s, (w, h) in enumerate(pairs):
                    last = nc.tensor.matmul(fc1_bank[k % 4], w1[:, w, m * P:(m + 1) * P], HTM[:, g, h, :],
                                            start=(s == 0), stop=(s == 3))
                last.then_inc(fc1_done, 1)

            def fc2(l, g, b, n):
                pe.wait_ge(gelu_done, MT * (NG * l + g + 1))
                if b == 0:
                    pe.wait_ge(w2_in, 96 * (l + 1))
                if n >= 2:
                    pe.wait_ge(mul2_done, n - 1)
                c = (b % GB) * T
                for m in range(MT):
                    last = nc.tensor.matmul((b5, b6)[n % 2][:, 0:C], GE[:, g, m, c:c + T], w2[:, m, :],
                                            start=(m == 0), stop=(m == MT - 1))
                last.then_inc(fc2_done, 1)

            for l in range(L):
                q0, n0 = 2 * B * l, B * l
                for i in range(-2, B + 2):
                    if 0 <= i + 1 < B:
                        if i + 1 >= 4:
                            pe.wait_ge(mul_done, n0 + i - 2)
                        transpose_h(q0 + i + 1, b4)
                    if 0 <= i < B:
                        scores_for_max(n0 + i, 0)
                    if 0 <= i + 1 < B:
                        qkv(l, i + 1, q0 + i + 1, n0 + i + 1)
                    if 0 <= i < B:
                        scores_for_max(n0 + i, 1)
                    if 0 <= i - 1 < B:
                        scores_less_max(n0 + i - 1, 0)
                    if 0 <= i + 1 < B:
                        transpose_qk(i + 1, n0 + i + 1)
                    if 0 <= i - 1 < B:
                        scores_less_max(n0 + i - 1, 1)
                        values(i - 1, n0 + i - 1, 0)
                    if 0 <= i - 2 < B:
                        transpose_o(n0 + i - 2)
                    if 0 <= i < B:
                        transpose_q2(i, n0 + i)
                    if 0 <= i - 1 < B:
                        values(i - 1, n0 + i - 1, 1)
                    if 0 <= i - 2 < B:
                        project(l, n0 + i - 2)
                    if 0 <= i - 1 < B:
                        transpose_ot(i - 1, n0 + i - 1)
                qm = q0 + B
                for b in range(GB):
                    transpose_hm(l, b, qm + b, n0 + b)
                for m in range(MT):
                    fc1(l, 0, m)
                    if m < GB:
                        transpose_hm(l, GB + m, qm + GB + m, n0 + GB + m)
                for m in range(MT):
                    fc1(l, 1, m)
                    if m < GB:
                        fc2(l, 0, m, n0 + m)
                for b in range(GB, B):
                    fc2(l, 1, b, n0 + b)


def kernel(**inputs):
    import numpy as np
    import concourse.bacc as bacc
    from concourse import mybir as mb
    from concourse.bass_utils import run_bass_kernel_spmd as run

    def by_layer(a, b):
        return np.stack([np.asarray(inputs["L0_cond_" + a]), np.asarray(inputs["L1_cond_" + b])])

    x = np.ascontiguousarray(inputs["x"])
    rest = x.shape[2] - 128
    row_marks = np.zeros((128, 2), np.float32)
    row_marks[2 * rest:3 * rest, 0] = 1.0
    row_marks[3 * rest + 1, 0] = 1.0
    row_marks[rest, 1] = 1.0
    arrays = {
        "x": x,
        "cond_t": np.ascontiguousarray(np.asarray(inputs["cond_1152"]).T),
        "w_ada": by_layer("W_ada", "ada_w"), "b_ada": by_layer("b_ada", "ada_b"),
        "w_qkv": by_layer("W_qkv", "qkv_w"), "b_qkv": by_layer("b_qkv", "qkv_b"),
        "w_proj": by_layer("W_proj", "out_w"), "b_proj": by_layer("b_proj", "out_b"),
        "w_fc1": by_layer("W_fc1", "w1"), "b_fc1": by_layer("b_fc1", "b1"),
        "w_fc2": by_layer("W_fc2", "w2"), "b_fc2": by_layer("b_fc2", "b2"),
        "identity": np.eye(128, dtype=np.float32),
        "row_marks": row_marks,
    }
    nc = bacc.Bacc("TRN2", target_bir_lowering=False, num_devices=1)
    aps = {k: nc.dram_tensor(f"in_{k}", a.shape, mb.dt.from_np(a.dtype), kind="ExternalInput").ap()
           for k, a in arrays.items()}
    out = nc.dram_tensor("out_x", x.shape, mb.dt.from_np(x.dtype), kind="ExternalOutput").ap()
    dit_two_blocks(nc, *aps.values(), out)
    r = run(nc, [{f"in_{k}": a for k, a in arrays.items()}], core_ids=[0])
    return r.results[0]["out_x"]
```

```python
import concourse.bass as bass
from concourse import mybir
from contextlib import ExitStack


def dit_two_blocks(nc, x, cond_t, w_ada, w_qkv, w_proj, w_fc1, w_fc2, marks, out):
    F32 = mybir.dt.float32
    F32R = mybir.dt.float32r
    ALU = mybir.AluOpType
    ACT = mybir.ActivationFunctionType
    AX = mybir.AxisListType

    B, T, C = x.shape
    L = w_qkv.shape[0]
    P = 128
    H = 16
    D = C // H
    R = C - P
    F = w_fc1.shape[2]
    MT = -(-F // P)
    FR = F - (MT - 1) * P
    HP = P // 4
    G = H // 4
    GB = 4
    NG = B // GB
    BANK = 512
    HALF = H * T // 2
    EPS = 1e-6
    SCALE = 1.0 / 3.0
    ADA = 6 * C
    LO_R, HI_R, ONES, LO_A = C, C + R, C + 2 * R, 2 * P
    MAX_HI, MAX_LO = 3 * D, 3 * D + 1

    ctx = ExitStack()
    with ctx:
        def sb(name, shape, dt=F32):
            return ctx.enter_context(nc.sbuf_tensor(name, shape, dt))

        def sem(name):
            return ctx.enter_context(nc.semaphore(name))

        X = sb("X", [P, B, C])
        MOD1 = sb("MOD1", [P, B, 3 * C])
        MOD2 = sb("MOD2", [P, B, 3 * C])
        consts = sb("consts", [P, P + 1])
        ident, low_row = consts[:, 0:P], consts[:, P:P + 1]
        ident_r = sb("ident_r", [P, P], F32R)
        cT = sb("cT", [P, 2, B])
        ce = sb("ce", [P, 2, B])
        cr = sb("cr", [P, 2, B])
        cs = sb("cs", [P, 2, B])
        wada = sb("wada", [P, 2, ADA])
        ada = sb("ada", [B, L, ADA])
        raw_q = sb("raw_q", [P, 2, 3 * C])
        wq = sb("wq", [P, 3, 3 * C], F32R)
        raw_1 = sb("raw_1", [P, 2, MT * P])
        w1 = sb("w1", [P, 3, MT * P], F32R)
        split_hi = sb("split_hi", [P, MT * P], F32R)
        split_lo = sb("split_lo", [P, MT * P])
        w2 = sb("w2", [P, MT, C])
        wp = sb("wp", [P, 2, C])
        bst = sb("bst", [P, 2, 6])
        mv = sb("mv", [P, 2, 2])
        veps = sb("veps", [P, 2])
        rstd = sb("rstd", [P, 2])
        shift0 = sb("shift0", [P, 2])
        mhalf = sb("mhalf", [P, 1])
        h1 = sb("h1", [P, C])
        h2 = sb("h2", [P, C])
        h1m = sb("h1m", [P, C])
        hf = sb("hf", [P, 2, C])
        HS = sb("HS", [P, 2, 3 * P], F32R)
        HT = sb("HT", [P, 3, T], F32R)
        HTM = sb("HTM", [P, NG, 3, GB * T], F32R)
        QK = sb("QK", [P, 3, 2, H * HP], F32R)
        V = sb("V", [P, 4, H * HP])
        KT = sb("KT", [P, 2, G * T], F32R)
        Q1T = sb("Q1T", [P, 2, G * T], F32R)
        Q2T = sb("Q2T", [P, G * T], F32R)
        KBD = sb("KBD", [P, 3, G, 4 * T], F32R)
        nm = sb("nm", [P, H])
        Pr = sb("Pr", [P, H * T])
        OT = sb("OT", [P, G * T])
        rs = sb("rs", [P, H])
        o = sb("o", [P, 2 * P])
        oT = sb("oT", [P, 2, T])
        tmp = sb("tmp", [P, 2, C])
        tmp2 = sb("tmp2", [P, 2, C])
        GE = sb("GE", [P, NG, MT, GB * T])

        S1 = ctx.enter_context(nc.psum_tensor("S1", [P, 2 * BANK], F32))
        S2 = ctx.enter_context(nc.psum_tensor("S2", [P, 2 * BANK], F32))
        b4, b5, b6, b7 = (ctx.enter_context(nc.psum_tensor(f"bank{i}", [P, BANK], F32)) for i in (4, 5, 6, 7))
        fc1_bank = [S1[:, 0:BANK], S1[:, BANK:], S2[:, 0:BANK], S2[:, BANK:]]
        ada_dram = nc.dram_tensor("ada_scratch", (L, B, ADA), F32, kind="Internal").ap()

        x_in = [sem("x_first_in"), sem("x_rest_in")]
        const_in = sem("const_in")
        cond_in = sem("cond_in")
        wada_in = sem("wada_in")
        raw_q_in = sem("raw_q_in")
        raw_1_in = sem("raw_1_in")
        w2_in = sem("w2_in")
        wp_in = sem("wp_in")
        mod1_first_in = sem("mod1_first_in")
        mod1_in = sem("mod1_in")
        mod2_in = sem("mod2_in")
        kbd_in = [sem(f"kbd{i}_in") for i in range(3)]
        out_done = sem("out_done")
        ada_out = sem("ada_out")
        dve_step = sem("dve_step")
        pool_step = sem("pool_step")
        cleared = sem("cleared")
        pool_cleared = sem("pool_cleared")
        dve_cleared = sem("dve_cleared")
        silu_e = sem("silu_e")
        silu_done = sem("silu_done")
        ident_ready = sem("ident_ready")
        ada_mm = sem("ada_mm")
        ada_ready = sem("ada_ready")
        wq_hi = sem("wq_hi")
        wq_ready = sem("wq_ready")
        w1_hi = sem("w1_hi")
        w1_ready = sem("w1_ready")
        stats_done = sem("stats_done")
        rstd_done = sem("rstd_done")
        h_ready = sem("h_ready")
        hs_hi = sem("hs_hi")
        hs_lo = sem("hs_lo")
        t1_done = sem("t1_done")
        ht_evac = sem("ht_evac")
        qkv_done = sem("qkv_done")
        split_done = sem("split_done")
        lo_done = sem("lo_done")
        tk_done = sem("tk_done")
        tq_done = sem("tq_done")
        kt_evac = sem("kt_evac")
        q1_evac = sem("q1_evac")
        s1_done = [sem("s1a_done"), sem("s1b_done")]
        max_done = [sem("maxa_done"), sem("maxb_done")]
        nm_done = sem("nm_done")
        t3_done = sem("t3_done")
        q2_evac = sem("q2_evac")
        s2_done = [sem("s2a_done"), sem("s2b_done")]
        exp_done = [sem("expa_done"), sem("expb_done")]
        pv_done = [sem("pva_done"), sem("pvb_done")]
        ot_evac = sem("ot_evac")
        t4_done = sem("t4_done")
        norm_done = sem("norm_done")
        t5_done = sem("t5_done")
        o_evac = sem("o_evac")
        proj_done = sem("proj_done")
        mul_done = sem("mul_done")
        x1_done = sem("x1_done")
        fc1_done = sem("fc1_done")
        gelu_done = sem("gelu_done")
        fc2_done = sem("fc2_done")
        mul2_done = sem("mul2_done")
        x2_done = sem("x2_done")

        def fc2_bank(b):
            return b7 if b < GB and b % 2 else b4

        def heads(ap):
            return ap.rearrange("p (h r) -> p h r", r=HP)

        FIRST, LAST = -3, B + 1

        block = ctx.enter_context(nc.Block())

        @block.sync
        def _(sp):
            def load(to, frm, s):
                sp.dma_start(to, frm).then_inc(s, 16)

            def load_split(raw, w, l, n, s):
                load(raw[:, 0, 0:n], w[l, 0:P, :], s)
                load(raw[0:w.shape[1] - P, 1, 0:n], w[l, P:, :], s)

            def load_ada(l):
                load(wada[:, 0, :], w_ada[l, 0:P, :], wada_in)
                load(wada[0:R + 1, 1, :], w_ada[l, P:C + 1, :], wada_in)

            def mods(l, b0, b1, half):
                return ada_dram[l, b0:b1, half * 3 * C:(half + 1) * 3 * C].partition_broadcast(P)

            def load_attention(l):
                if l > 0:
                    sp.wait_ge(wq_ready, l)
                load_split(raw_q, w_qkv, l, 3 * C, raw_q_in)
                if l > 0:
                    sp.wait_ge(proj_done, B * l)
                load(wp[:, 0, :], w_proj[l, 0:P, :], wp_in)
                load(wp[0:R + 1, 1, :], w_proj[l, P:C + 1, :], wp_in)

            def load_mlp(l):
                if l > 0:
                    sp.wait_ge(w1_ready, l)
                load_split(raw_1, w_fc1, l, F, raw_1_in)
                if l > 0:
                    sp.wait_ge(fc2_done, B * l)
                load(w2[:, 0:MT - 1, :], w_fc2[l, 0:(MT - 1) * P, :].rearrange("(m p) c -> p m c", p=P), w2_in)
                load(w2[0:FR + 1, MT - 1, :], w_fc2[l, (MT - 1) * P:F + 1, :], w2_in)

            load(cT[:, 0, :], cond_t[0:P, :], cond_in)
            load(cT[0:R, 1, :], cond_t[P:C, :], cond_in)
            load_ada(0)
            load(consts[:], marks, const_in)
            load(X[:, 0, :], x[0, :, :], x_in[0])
            sp.wait_ge(cleared, 1)
            load_attention(0)
            sp.wait_ge(ada_mm, 1)
            load_ada(1)
            sp.wait_ge(ada_ready, 1)
            load(ada_dram[0, :, :], ada[:, 0, :], ada_out)
            sp.wait_ge(ada_out, 16)
            load(MOD1[:, 0:1, :], mods(0, 0, 1, 0), mod1_first_in)
            load(MOD1[:, 1:B, :], mods(0, 1, B, 0), mod1_in)
            load(X[:, 1:B, :], x[1:B, :, :].rearrange("b t c -> t b c"), x_in[1])
            sp.wait_ge(cleared, 2)
            load_mlp(0)
            load(MOD2[:, :, :], mods(0, 0, B, 1), mod2_in)

            def move_k(n):
                sp.wait_ge(kt_evac, n + 1)
                if n >= 3:
                    sp.wait_ge(s2_done[1], n - 2)
                for j in range(4):
                    r = slice(HP * j, HP * (j + 1))
                    load(KBD[r, n % 3, :, j * T:(j + 1) * T].bitcast(F32),
                         KT[r, n % 2, :].rearrange("p (g t) -> p g t", g=G).bitcast(F32), kbd_in[n % 3])

            for l in range(L):
                for b in range(B):
                    move_k(B * l + b)
                    if l == 0 and b == 0:
                        sp.wait_ge(ada_ready, 2)
                        load(ada_dram[1, :, :], ada[:, 1, :], ada_out)
                if l + 1 < L:
                    sp.wait_ge(ada_out, 32)
                    load_attention(l + 1)
                    sp.wait_ge(mul_done, B * (l + 1))
                    load(MOD1[:, :, :], mods(l + 1, 0, B, 0), mod1_in)
                    load_mlp(l + 1)
                    sp.wait_ge(mul2_done, B * (l + 1))
                    load(MOD2[:, :, :], mods(l + 1, 0, B, 1), mod2_in)
            for b in range(B):
                sp.wait_ge(x2_done, B * (L - 1) + b + 1)
                load(out[b, :, :], X[:, b, :], out_done)
            sp.wait_ge(out_done, 16 * B)

        @block.gpsimd
        def _(pool):
            steps = [0]

            def link(ins):
                steps[0] += 1
                ins.then_inc(pool_step, 1)
                pool.wait_ge(pool_step, steps[0])

            def low_weights(l, raw, w, n, hi, ready):
                pool.wait_ge(hi, l + 1)
                link(nc.gpsimd.tensor_scalar(split_lo[:, 0:n], split_hi[:, 0:n].bitcast(F32), low_row, 1.0,
                                             ALU.mult, ALU.mult))
                nc.gpsimd.tensor_tensor(w[:, 2, 0:n], raw[:, 1, 0:n], split_lo[:, 0:n], ALU.subtract)
                nc.gpsimd.tensor_tensor(w[:, 1, 0:n], raw[:, 0, 0:n], w[:, 0, 0:n].bitcast(F32),
                                        ALU.subtract).then_inc(ready, 1)

            def inv_std(q):
                pool.wait_ge(stats_done, q + 1)
                link(nc.gpsimd.tensor_scalar(veps[:, q % 2:q % 2 + 1], mv[:, q % 2, 1:2], 1.0, EPS, ALU.mult, ALU.add))
                nc.gpsimd.tensor_tensor(rstd[:, q % 2:q % 2 + 1], veps[:, q % 2:q % 2 + 1], mhalf[:],
                                        ALU.pow).then_inc(rstd_done, 1)

            def modulate(q, l, b):
                k = slice(q % 2, q % 2 + 1)
                pool.wait_ge(rstd_done, q + 1)
                link(nc.gpsimd.tensor_scalar(shift0[:, k], mv[:, q % 2, 0:1], rstd[:, k], -1.0, ALU.mult, ALU.mult))
                link(nc.gpsimd.tensor_scalar(h1[:], X[:, b, :], rstd[:, k], shift0[:, k], ALU.mult, ALU.add))
                if l == 0 and b == 0:
                    pool.wait_ge(mod1_first_in, 16)
                else:
                    pool.wait_ge(mod1_in, 16 * (l + 1))
                link(nc.gpsimd.tensor_tensor(h2[:], h1[:], MOD1[:, b, C:2 * C], ALU.mult))
                nc.gpsimd.tensor_tensor(hf[:, q % 2, :], h2[:], MOD1[:, b, 0:C], ALU.add).then_inc(h_ready, 1)

            def low_part(q):
                hs, h = HS[:, q % 2, :], hf[:, q % 2, :]
                pool.wait_ge(hs_hi, q + 1)
                nc.gpsimd.tensor_tensor(hs[:, LO_A:LO_A + P], h[:, 0:P], hs[:, 0:P].bitcast(F32), ALU.subtract)
                nc.gpsimd.tensor_tensor(hs[:, LO_R:LO_R + R], h[:, P:C], hs[:, P:C].bitcast(F32), ALU.subtract)
                nc.gpsimd.tensor_copy(hs[:, HI_R:HI_R + R], hs[:, P:C].bitcast(F32)).then_inc(hs_lo, 1)

            def add_residual(n, b):
                pool.wait_ge(mul_done, n + 1)
                nc.gpsimd.tensor_tensor(X[:, b, :], X[:, b, :], tmp[:, n % 2, :], ALU.add).then_inc(x1_done, 1)

            nc.gpsimd.memset(mhalf[:], -0.5)
            nc.gpsimd.memset(V[:], 0.0).then_inc(pool_cleared, 1)
            nc.gpsimd.memset(GE[:, :, MT - 1, :], 1.0).then_inc(pool_cleared, 1)
            pool.wait_ge(const_in, 16)
            low_weights(0, raw_q, wq, 3 * C, wq_hi, wq_ready)
            for l in range(L):
                q0, n0 = 2 * B * l, B * l
                for i in range(FIRST, LAST + 1):
                    q = q0 + i + 3
                    inv_std(q)
                    if i + 3 < B:
                        modulate(q, l, i + 3)
                    low_part(q)
                    if 0 <= i - 3 < B:
                        add_residual(n0 + i - 3, i - 3)
                    if i == 2:
                        low_weights(l, raw_1, w1, MT * P, w1_hi, w1_ready)
                add_residual(n0 + B - 1, B - 1)
                for b in range(LAST - FIRST + 1 - B, B):
                    inv_std(q0 + B + b)
                    low_part(q0 + B + b)
                if l + 1 < L:
                    low_weights(l + 1, raw_q, wq, 3 * C, wq_hi, wq_ready)

        @block.scalar
        def _(act):
            def high_weights(l, raw, w, n, arrived, hi):
                act.wait_ge(arrived, 32 * (l + 1))
                nc.scalar.copy(w[:, 0, 0:n], raw[:, 0, 0:n])
                nc.scalar.copy(split_hi[:, 0:n], raw[:, 1, 0:n]).then_inc(hi, 1)

            def high_part(q):
                act.wait_ge(h_ready, q + 1)
                if q >= 2:
                    act.wait_ge(t1_done, q - 1)
                nc.scalar.copy(HS[:, q % 2, 0:C], hf[:, q % 2, :]).then_inc(hs_hi, 1)

            def evac_ht(q, n):
                act.wait_ge(t1_done, q + 1)
                if n > 0:
                    act.wait_ge(qkv_done, n)
                nc.scalar.copy(HT[:].rearrange("p k t -> p (k t)"), b5[:, 0:3 * T]).then_inc(ht_evac, 1)

            def split_qkv(n):
                act.wait_ge(qkv_done, n + 1)
                if n >= 3:
                    act.wait_ge(t3_done, n - 2)
                if n >= 4:
                    act.wait_ge(pv_done[1], n - 3)
                for k, slot in ((0, 0), (1, D)):
                    src = b5[:, k * C:(k + 1) * C].rearrange("p (h d) -> p h d", d=D)
                    dst = heads(QK[:, n % 3, k, :])[:, :, slot:slot + 2 * D].rearrange("p h (s d) -> p h s d", d=D)
                    nc.scalar.copy(dst, src.unsqueeze(2).broadcast_to([P, H, 2, D]))
                nc.scalar.copy(heads(V[:, n % 4, :])[:, :, 0:D],
                               b5[:, 2 * C:3 * C].rearrange("p (h d) -> p h d", d=D)).then_inc(split_done, 1)

            def evac_q1(n):
                act.wait_ge(tq_done, n + 1)
                if n >= 2:
                    act.wait_ge(s1_done[1], n - 1)
                nc.scalar.copy(Q1T[:, n % 2, :], b7[:]).then_inc(q1_evac, 1)

            def evac_q2(n):
                act.wait_ge(t3_done, n + 1)
                if n > 0:
                    act.wait_ge(s2_done[1], n)
                nc.scalar.copy(Q2T[:], b6[:]).then_inc(q2_evac, 1)

            def exp_half(n, half):
                act.wait_ge(s2_done[half], n + 1)
                if n > 0:
                    act.wait_ge(pv_done[half], n)
                nc.scalar.activation(Pr[:, half * HALF:(half + 1) * HALF], S2[:], ACT.Exp,
                                     scale=SCALE).then_inc(exp_done[half], 1)

            def evac_ot(n):
                act.wait_ge(pv_done[1], n + 1)
                if n > 0:
                    act.wait_ge(t4_done, n)
                nc.scalar.copy(OT[:], b7[:]).then_inc(ot_evac, 1)

            def evac_o(n):
                act.wait_ge(t5_done, n + 1)
                if n > 0:
                    act.wait_ge(proj_done, n)
                nc.scalar.copy(oT[:].rearrange("p k t -> p (k t)"), b4[:, 0:2 * T]).then_inc(o_evac, 1)

            def evac_htm(q, n):
                act.wait_ge(t1_done, q + 1)
                gg, g, c = n // GB, n // GB % NG, n % GB * T
                if gg >= NG:
                    act.wait_ge(fc1_done, MT * (gg - 1))
                nc.scalar.copy(HTM[:, g, :, c:c + T],
                               b5[:, 0:3 * T].rearrange("p (k t) -> p k t", k=3)).then_inc(ht_evac, 1)

            def gelu(gg, g, m):
                act.wait_ge(fc1_done, MT * gg + m + 1)
                if gg >= NG:
                    act.wait_ge(fc2_done, GB * (gg - 1))
                rows = P if m < MT - 1 else FR
                nc.scalar.activation(GE[0:rows, g, m, :], fc1_bank[(MT * gg + m) % 4][0:rows, :],
                                     ACT.Gelu_apprx_tanh).then_inc(gelu_done, 1)

            act.wait_ge(cond_in, 32)
            nc.scalar.activation(ce[:, 0, :], cT[:, 0, :], ACT.Exp, scale=-1.0)
            nc.scalar.activation(ce[0:R, 1, :], cT[0:R, 1, :], ACT.Exp, scale=-1.0).then_inc(silu_e, 1)
            high_weights(0, raw_q, wq, 3 * C, raw_q_in, wq_hi)
            act.wait_ge(dve_cleared, 1)
            act.wait_ge(pool_cleared, 2)
            for l in range(L):
                q0, n0 = 2 * B * l, B * l
                for i in range(FIRST, LAST + 1):
                    if 0 <= i + 2 < B:
                        evac_ht(q0 + i + 2, n0 + i + 2)
                    elif B <= i + 2:
                        evac_htm(q0 + i + 2, n0 + i + 2 - B)
                    if 0 <= i + 1 < B:
                        evac_q1(n0 + i + 1)
                    if 0 <= i - 1 < B:
                        exp_half(n0 + i - 1, 0)
                    if 0 <= i - 2 < B:
                        evac_o(n0 + i - 2)
                    if 0 <= i + 2 < B:
                        split_qkv(n0 + i + 2)
                    high_part(q0 + i + 3)
                    if 0 <= i - 1 < B:
                        exp_half(n0 + i - 1, 1)
                    if 0 <= i < B:
                        evac_q2(n0 + i)
                    if 0 <= i - 1 < B:
                        evac_ot(n0 + i - 1)
                    if i == 2:
                        high_weights(l, raw_1, w1, MT * P, raw_1_in, w1_hi)
                for m in range(MT):
                    gelu(NG * l, 0, m)
                    if m < GB:
                        evac_htm(q0 + B + GB + m, n0 + GB + m)
                        if GB + m + 1 < B:
                            high_part(q0 + B + GB + m + 1)
                if l + 1 < L:
                    high_weights(l + 1, raw_q, wq, 3 * C, raw_q_in, wq_hi)
                for m in range(MT):
                    gelu(NG * l + 1, 1, m)

        @block.vector
        def _(dve):
            steps = [0]

            def link(ins):
                steps[0] += 1
                ins.then_inc(dve_step, 1)
                dve.wait_ge(dve_step, steps[0])

            def finish_ada(l):
                dve.wait_ge(ada_mm, l + 1)
                for k in range(2):
                    bank = (b4, b5)[k] if l == 0 else (b6, b7)[k]
                    link(nc.vector.tensor_copy(ada[:, l, 3 * C * k:3 * C * (k + 1)], bank[0:B, 0:3 * C]))
                v = ada[:, l, :].rearrange("b (k c) -> b k c", k=2)[:, :, C:2 * C]
                nc.vector.tensor_scalar_add(v, v, 1.0).then_inc(ada_ready, 1)

            def norm_stats(q, b):
                if q >= 2:
                    dve.wait_ge(h_ready, q - 1)
                link(nc.vector.bn_stats(bst[:, q % 2, :], X[:, b, :]))
                nc.vector.bn_aggr(mv[:, q % 2, :], bst[:, q % 2, :]).then_inc(stats_done, 1)

            def modulate(q, l, b):
                dve.wait_ge(stats_done, q + 1)
                dve.wait_ge(mod2_in, 16 * (l + 1))
                link(nc.vector.scalar_tensor_tensor(out=h1m[:], in0=X[:, b, :], scalar=mv[:, q % 2, 0:1],
                                                    in1=MOD2[:, b, C:2 * C],
                                                    op0=ALU.subtract, op1=ALU.mult))
                dve.wait_ge(rstd_done, q + 1)
                dve.wait_ge(hs_lo, q - 1)
                nc.vector.scalar_tensor_tensor(out=hf[:, q % 2, :], in0=h1m[:], scalar=rstd[:, q % 2:q % 2 + 1],
                                               in1=MOD2[:, b, 0:C],
                                               op0=ALU.mult, op1=ALU.add).then_inc(h_ready, 1)

            def low_qk(n):
                dve.wait_ge(split_done, n + 1)
                for k, slot in ((0, 2 * D), (1, 0)):
                    v = heads(QK[:, n % 3, k, :])
                    nc.vector.tensor_tensor(v[:, :, slot:slot + D],
                                            b5[:, k * C:(k + 1) * C].rearrange("p (h d) -> p h d", d=D),
                                            v[:, :, D:2 * D].bitcast(F32), ALU.subtract)
                nc.vector.memset(heads(QK[:, n % 3, 0, :])[:, :, MAX_HI:MAX_LO + 1].bitcast(F32),
                                 0.0).then_inc(lo_done, 1)

            def evac_kt(n):
                dve.wait_ge(tk_done, n + 1)
                if n >= 2:
                    dve.wait_ge(kbd_in[(n - 2) % 3], 64 * ((n - 2) // 3 + 1))
                nc.vector.tensor_copy(KT[:, n % 2, :], b6[:]).then_inc(kt_evac, 1)

            def neg_max(n, half):
                dve.wait_ge(s1_done[half], n + 1)
                nc.vector.tensor_reduce(nm[:, half * H // 2:(half + 1) * H // 2],
                                        S1[:].rearrange("p (h t) -> p h t", t=T), AX.X, ALU.max,
                                        negate=True).then_inc(max_done[half], 1)

            def split_max(n):
                v = heads(QK[:, n % 3, 0, :])
                m = nm[:].unsqueeze(2)
                dve.wait_ge(max_done[1], n + 1)
                link(nc.vector.tensor_copy(v[:, :, MAX_HI:MAX_HI + 1], m))
                nc.vector.tensor_tensor(v[:, :, MAX_LO:MAX_LO + 1], m, v[:, :, MAX_HI:MAX_HI + 1].bitcast(F32),
                                        ALU.subtract).then_inc(nm_done, 1)

            def normalise(n):
                v = heads(b4[:])
                dve.wait_ge(t4_done, n + 1)
                link(nc.vector.reciprocal(rs[:].unsqueeze(2), v[:, :, D:D + 1]))
                if n > 0:
                    dve.wait_ge(t5_done, n)
                nc.vector.tensor_tensor(o[:, 0:C].rearrange("p (h d) -> p h d", d=D), v[:, :, 0:D],
                                        rs[:].unsqueeze(2).broadcast_to([P, H, D]), ALU.mult).then_inc(norm_done, 1)

            def gate(n, b):
                dve.wait_ge(proj_done, n + 1)
                if n >= 2:
                    dve.wait_ge(x1_done, n - 1)
                nc.vector.tensor_tensor(tmp[:, n % 2, :], b4[:, 2 * T:2 * T + C], MOD1[:, b, 2 * C:3 * C],
                                        ALU.mult).then_inc(mul_done, 1)

            def residual2(n, b):
                dve.wait_ge(fc2_done, n + 1)
                nc.vector.tensor_tensor(tmp2[:, n % 2, :], fc2_bank(b)[:, 0:C], MOD2[:, b, 2 * C:3 * C],
                                        ALU.mult).then_inc(mul2_done, 1)
                dve.wait_ge(mul2_done, n + 1)
                nc.vector.tensor_tensor(X[:, b, :], X[:, b, :], tmp2[:, n % 2, :], ALU.add).then_inc(x2_done, 1)

            nc.vector.memset(cs[:, 1, :], 1.0)
            dve.wait_ge(cond_in, 32)
            dve.wait_ge(silu_e, 1)
            for r, k in ((P, 0), (R, 1)):
                link(nc.vector.tensor_scalar_add(ce[0:r, k, :], ce[0:r, k, :], 1.0))
                link(nc.vector.reciprocal(cr[0:r, k, :], ce[0:r, k, :]))
                last = nc.vector.tensor_tensor(cs[0:r, k, :], cT[0:r, k, :], cr[0:r, k, :], ALU.mult)
            last.then_inc(silu_done, 1)
            nc.vector.memset(raw_q[:, 1, :], 0.0).then_inc(cleared, 1)
            nc.vector.memset(QK[:].bitcast(F32), 0.0)
            dve.wait_ge(const_in, 16)
            nc.vector.tensor_copy(ident_r[:], ident).then_inc(ident_ready, 1)
            finish_ada(0)
            link(nc.vector.memset(HS[:].bitcast(F32), 0.0))
            nc.vector.memset(HS[:, :, ONES:ONES + 2].bitcast(F32), 1.0).then_inc(dve_cleared, 1)
            nc.vector.memset(raw_1[:], 0.0).then_inc(cleared, 1)
            for third in range(3):
                nc.vector.memset(heads(QK[:, third, 1, :])[:, :, MAX_HI:MAX_LO + 1].bitcast(F32), 1.0)
            link(nc.vector.memset(o[:], 0.0))
            nc.vector.memset(o[:, C:C + 1], 1.0)
            dve.wait_ge(pool_cleared, 1)
            nc.vector.memset(V[:].rearrange("p a (h r) -> p (a h) r", r=HP)[:, :, D:D + 1], 1.0)
            nc.vector.memset(KBD[:].bitcast(F32), 0.0).then_inc(dve_cleared, 1)
            for l in range(L):
                q0, n0 = 2 * B * l, B * l
                for i in range(FIRST, LAST + 1):
                    q = q0 + i + 3
                    if i + 3 < B:
                        b = i + 3
                        if l == 0:
                            dve.wait_ge(x_in[min(b, 1)], 16)
                        else:
                            dve.wait_ge(x2_done, n0 - B + b + 1)
                        norm_stats(q, b)
                    else:
                        b = i + 3 - B
                        dve.wait_ge(x1_done, n0 + b + 1)
                        norm_stats(q, b)
                    if 0 <= i - 3 < B:
                        gate(n0 + i - 3, i - 3)
                    if 0 <= i + 1 < B:
                        evac_kt(n0 + i + 1)
                    if l > 0 and i <= 0:
                        residual2(n0 - GB + i + 3, GB + i + 3)
                    if 0 <= i < B:
                        neg_max(n0 + i, 0)
                    if 0 <= i - 2 < B:
                        normalise(n0 + i - 2)
                    if i + 3 >= B:
                        modulate(q, l, i + 3 - B)
                    if 0 <= i < B:
                        neg_max(n0 + i, 1)
                        split_max(n0 + i)
                    if 0 <= i + 2 < B:
                        low_qk(n0 + i + 2)
                    if l == 0 and i == FIRST:
                        finish_ada(1)
                gate(n0 + B - 1, B - 1)
                for b in range(LAST - FIRST + 1 - B, B):
                    dve.wait_ge(x1_done, n0 + b + 1)
                    norm_stats(q0 + B + b, b)
                    modulate(q0 + B + b, l, b)
                for b in range(GB if l + 1 < L else B):
                    residual2(n0 + b, b)

        @block.tensor
        def _(pe):
            def transpose_h(q):
                pe.wait_ge(hs_lo, q + 1)
                for k in range(3):
                    last = nc.tensor.transpose(b5[:, k * T:(k + 1) * T].bitcast(F32R),
                                               HS[:, q % 2, k * P:(k + 1) * P], ident_r[:])
                last.then_inc(t1_done, 1)

            def qkv(l, b, q, n):
                if b == 0:
                    pe.wait_ge(wq_ready, l + 1)
                pe.wait_ge(ht_evac, q + 1)
                pairs = ((0, 0), (0, 1), (1, 2), (2, 0))
                for k, (h, w) in enumerate(pairs):
                    last = nc.tensor.matmul(b5[:, 0:3 * C], HT[:, h, :], wq[:, w, :], start=(k == 0), stop=(k == 3))
                last.then_inc(qkv_done, 1)

            def transpose_qk(b, n):
                pe.wait_ge(lo_done, n + 1)
                if b >= 2:
                    pe.wait_ge(q2_evac, n - 1)
                if b == 1:
                    pe.wait_ge(kt_evac, n)
                for g in range(G):
                    last = nc.tensor.transpose(b6[:, g * T:(g + 1) * T].bitcast(F32R),
                                               QK[:, n % 3, 1, g * P:(g + 1) * P], ident_r[:])
                last.then_inc(tk_done, 1)
                if b >= 3:
                    pe.wait_ge(ot_evac, n - 2)
                elif b > 0:
                    pe.wait_ge(q1_evac, n)
                for g in range(G):
                    last = nc.tensor.transpose(b7[:, g * T:(g + 1) * T].bitcast(F32R),
                                               QK[:, n % 3, 0, g * P:(g + 1) * P], ident_r[:])
                last.then_inc(tq_done, 1)

            def scores_for_max(n, half):
                if half == 0:
                    pe.wait_ge(kbd_in[n % 3], 64 * (n // 3 + 1))
                    pe.wait_ge(q1_evac, n + 1)
                    if n > 0:
                        pe.wait_ge(max_done[1], n)
                else:
                    pe.wait_ge(max_done[0], n + 1)
                for k in range(2):
                    g = 2 * half + k
                    last = nc.tensor.matmul(S1[:, k * BANK:(k + 1) * BANK], Q1T[:, n % 2, g * T:(g + 1) * T],
                                            KBD[:, n % 3, g, :], start=True, stop=True)
                last.then_inc(s1_done[half], 1)

            def transpose_q2(b, n):
                pe.wait_ge(nm_done, n + 1)
                pe.wait_ge(kt_evac, n + 2 if b + 1 < B else n + 1)
                for g in range(G):
                    last = nc.tensor.transpose(b6[:, g * T:(g + 1) * T].bitcast(F32R),
                                               QK[:, n % 3, 0, g * P:(g + 1) * P], ident_r[:])
                last.then_inc(t3_done, 1)

            def scores_less_max(n, half):
                if half == 0:
                    pe.wait_ge(q2_evac, n + 1)
                    if n > 0:
                        pe.wait_ge(exp_done[1], n)
                else:
                    pe.wait_ge(exp_done[0], n + 1)
                for k in range(H // 2):
                    g, j = 2 * half + k // 4, k % 4
                    last = nc.tensor.matmul(S2[:, k * T:(k + 1) * T], KBD[:, n % 3, g, j * T:(j + 1) * T],
                                            Q2T[:, g * T:(g + 1) * T], start=True, stop=True)
                last.then_inc(s2_done[half], 1)

            def values(b, n, half):
                pe.wait_ge(exp_done[half], n + 1)
                if half == 0:
                    if b + 2 < B:
                        pe.wait_ge(q1_evac, n + 3)
                    elif n > 0:
                        pe.wait_ge(ot_evac, n)
                for h in range(half * H // 2, (half + 1) * H // 2):
                    g, j = h // 4, h % 4
                    last = nc.tensor.matmul(b7[HP * j:HP * (j + 1), g * T:(g + 1) * T],
                                            V[:, n % 4, HP * h:HP * (h + 1)], Pr[:, h * T:(h + 1) * T],
                                            start=True, stop=True)
                last.then_inc(pv_done[half], 1)

            def transpose_ot(l, b, n):
                pe.wait_ge(ot_evac, n + 1)
                if b > 0:
                    pe.wait_ge(mul_done, n)
                elif l > 0:
                    pe.wait_ge(mul2_done, n)
                for g in range(G):
                    last = nc.tensor.transpose(b4[:, g * T:(g + 1) * T], OT[:, g * T:(g + 1) * T], ident)
                last.then_inc(t4_done, 1)

            def transpose_o(n):
                pe.wait_ge(norm_done, n + 1)
                for k in range(2):
                    last = nc.tensor.transpose(b4[:, k * T:(k + 1) * T], o[:, k * P:(k + 1) * P], ident)
                last.then_inc(t5_done, 1)

            def project(l, b, n):
                pe.wait_ge(o_evac, n + 1)
                if b == 0:
                    pe.wait_ge(wp_in, 32 * (l + 1))
                for k, rows in enumerate((P, R + 1)):
                    last = nc.tensor.matmul(b4[:, 2 * T:2 * T + C], oT[0:rows, k, :], wp[0:rows, k, :],
                                            start=(k == 0), stop=(k == 1))
                last.then_inc(proj_done, 1)

            def fc1(l, g, m):
                k = MT * (NG * l + g) + m
                if m == 0:
                    pe.wait_ge(ht_evac, 2 * B * l + B + GB * (g + 1))
                    pe.wait_ge(w1_ready, l + 1)
                if k >= 4:
                    pe.wait_ge(gelu_done, k - 3)
                pairs = ((0, 0), (0, 2), (1, 0), (2, 1))
                for s, (w, h) in enumerate(pairs):
                    last = nc.tensor.matmul(fc1_bank[k % 4], w1[:, w, m * P:(m + 1) * P], HTM[:, g, h, :],
                                            start=(s == 0), stop=(s == 3))
                last.then_inc(fc1_done, 1)

            def fc2(l, b, n):
                g = b // GB
                pe.wait_ge(gelu_done, MT * (NG * l + g + 1))
                if b == 0:
                    pe.wait_ge(w2_in, 32 * (l + 1))
                    pe.wait_ge(mul_done, n + B)
                elif b >= GB:
                    pe.wait_ge(mul2_done, n)
                elif b >= 2:
                    pe.wait_ge(mul2_done, n - 1)
                c = (b % GB) * T
                for m in range(MT):
                    rows = P if m < MT - 1 else FR + 1
                    last = nc.tensor.matmul(fc2_bank(b)[:, 0:C], GE[0:rows, g, m, c:c + T], w2[0:rows, m, :],
                                            start=(m == 0), stop=(m == MT - 1))
                last.then_inc(fc2_done, 1)

            pe.wait_ge(silu_done, 1)
            for l in range(L):
                pe.wait_ge(wada_in, 32 * (l + 1))
                for k in range(2):
                    bank = (b4, b5)[k] if l == 0 else (b6, b7)[k]
                    cols = slice(3 * C * k, 3 * C * (k + 1))
                    nc.tensor.matmul(bank[0:B, 0:3 * C], cs[:, 0, :], wada[:, 0, cols], start=True, stop=False)
                    last = nc.tensor.matmul(bank[0:B, 0:3 * C], cs[0:R + 1, 1, :], wada[0:R + 1, 1, cols],
                                            start=False, stop=True)
                last.then_inc(ada_mm, 1)
            pe.wait_ge(ident_ready, 1)
            pe.wait_ge(dve_cleared, 1)
            pe.wait_ge(ada_ready, 1)
            for l in range(L):
                q0, n0 = 2 * B * l, B * l
                for i in range(FIRST, LAST + 1):
                    if i + 2 >= 0:
                        if 1 <= i + 2 <= B:
                            pe.wait_ge(lo_done, n0 + i + 2)
                        elif i + 2 > 0:
                            pe.wait_ge(ht_evac, q0 + i + 2)
                        transpose_h(q0 + i + 2)
                    if 0 <= i + 1 < B:
                        if l == 0 and i + 1 == 0:
                            pe.wait_ge(ada_ready, 2)
                            pe.wait_ge(dve_cleared, 2)
                        transpose_qk(i + 1, n0 + i + 1)
                    if l > 0 and i <= 0:
                        fc2(l - 1, GB + i + 3, n0 - GB + i + 3)
                    if 0 <= i < B:
                        scores_for_max(n0 + i, 0)
                    if 0 <= i - 2 < B:
                        transpose_ot(l, i - 2, n0 + i - 2)
                    if 0 <= i - 1 < B:
                        scores_less_max(n0 + i - 1, 0)
                    if 0 <= i < B:
                        scores_for_max(n0 + i, 1)
                    if 0 <= i - 2 < B:
                        transpose_o(n0 + i - 2)
                    if 0 <= i + 2 < B:
                        qkv(l, i + 2, q0 + i + 2, n0 + i + 2)
                    if 0 <= i - 1 < B:
                        scores_less_max(n0 + i - 1, 1)
                        values(i - 1, n0 + i - 1, 0)
                    if 0 <= i < B:
                        transpose_q2(i, n0 + i)
                    if 0 <= i - 1 < B:
                        values(i - 1, n0 + i - 1, 1)
                    if 0 <= i - 2 < B:
                        project(l, i - 2, n0 + i - 2)
                for m in range(MT):
                    fc1(l, 0, m)
                    if m < GB:
                        pe.wait_ge(ht_evac, q0 + B + GB + m)
                        transpose_h(q0 + B + GB + m)
                for m in range(MT):
                    fc1(l, 1, m)
                    if m < GB:
                        fc2(l, m, n0 + m)
            for b in range(GB, B):
                fc2(L - 1, b, B * (L - 1) + b)


def kernel(**inputs):
    import numpy as np
    import concourse.bacc as bacc
    from concourse import mybir as mb
    from concourse.bass_utils import run_bass_kernel_spmd as run

    def by_layer(names, rows):
        return np.stack([np.concatenate(rows(np.asarray(inputs[w]), np.asarray(inputs[b])[None, :])) for w, b in names])

    def plain(w, b):
        return [w, b]

    def stacked(w, b):
        return [w, w[128:], w[128:], b, b]

    x = np.ascontiguousarray(inputs["x"])
    rest = x.shape[2] - 128
    marks = np.zeros((128, 129), np.float32)
    marks[:, 0:128] = np.eye(128, dtype=np.float32)
    marks[2 * rest:3 * rest, 128] = 1.0
    marks[3 * rest + 1, 128] = 1.0
    arrays = {
        "x": x,
        "cond_t": np.ascontiguousarray(np.asarray(inputs["cond_1152"]).T),
        "w_ada": by_layer([("L0_cond_W_ada", "L0_cond_b_ada"), ("L1_cond_ada_w", "L1_cond_ada_b")], plain),
        "w_qkv": by_layer([("L0_cond_W_qkv", "L0_cond_b_qkv"), ("L1_cond_qkv_w", "L1_cond_qkv_b")], stacked),
        "w_proj": by_layer([("L0_cond_W_proj", "L0_cond_b_proj"), ("L1_cond_out_w", "L1_cond_out_b")], plain),
        "w_fc1": by_layer([("L0_cond_W_fc1", "L0_cond_b_fc1"), ("L1_cond_w1", "L1_cond_b1")], stacked),
        "w_fc2": by_layer([("L0_cond_W_fc2", "L0_cond_b_fc2"), ("L1_cond_w2", "L1_cond_b2")], plain),
        "marks": marks,
    }
    nc = bacc.Bacc("TRN2", target_bir_lowering=False, num_devices=1)
    aps = {k: nc.dram_tensor(f"in_{k}", a.shape, mb.dt.from_np(a.dtype), kind="ExternalInput").ap()
           for k, a in arrays.items()}
    out = nc.dram_tensor("out_x", x.shape, mb.dt.from_np(x.dtype), kind="ExternalOutput").ap()
    dit_two_blocks(nc, *aps.values(), out)
    r = run(nc, [{f"in_{k}": a for k, a in arrays.items()}], core_ids=[0])
    return r.results[0]["out_x"]
```

```python
import concourse.bass as bass
from concourse import mybir
from contextlib import ExitStack


def dit_two_blocks(nc, x, cond_t, w_ada, w_qkv, w_proj, w_fc1, w_fc2, marks, out):
    F32 = mybir.dt.float32
    F32R = mybir.dt.float32r
    ALU = mybir.AluOpType
    ACT = mybir.ActivationFunctionType
    AX = mybir.AxisListType

    B, T, C = x.shape
    L = w_qkv.shape[0]
    P = 128
    H = 16
    D = C // H
    R = C - P
    F = w_fc1.shape[2]
    MT = -(-F // P)
    FR = F - (MT - 1) * P
    HP = P // 4
    G = H // 4
    GB = 4
    NG = B // GB
    BANK = 512
    HALF = H * T // 2
    EPS = 1e-6
    SCALE = 1.0 / 3.0
    ADA = 6 * C
    AC = ADA // 4
    LO_R, HI_R, ONES, LO_A = C, C + R, C + 2 * R, 2 * P
    MAX_HI, MAX_LO = 3 * D, 3 * D + 1

    ctx = ExitStack()
    with ctx:
        def sb(name, shape, dt=F32):
            return ctx.enter_context(nc.sbuf_tensor(name, shape, dt))

        def sem(name):
            return ctx.enter_context(nc.semaphore(name))

        X = sb("X", [P, B, C])
        MOD1 = sb("MOD1", [P, B, 3 * C])
        MOD2 = sb("MOD2", [P, B, 3 * C])
        consts = sb("consts", [P, P + 1])
        ident, low_row = consts[:, 0:P], consts[:, P:P + 1]
        ident_r = sb("ident_r", [P, P], F32R)
        cT = sb("cT", [P, 2, B])
        ce = sb("ce", [P, 2, B])
        cr = sb("cr", [P, 2, B])
        cs = sb("cs", [P, 2, HP])
        wada = sb("wada", [P, L, 2, ADA])
        ada = sb("ada", [P, L, AC])
        raw_q = sb("raw_q", [P, 2, 3 * C])
        wq = sb("wq", [P, 3, 3 * C], F32R)
        raw_1 = sb("raw_1", [P, 2, MT * P])
        w1 = sb("w1", [P, 3, MT * P], F32R)
        split_hi = sb("split_hi", [P, MT * P], F32R)
        split_lo = sb("split_lo", [P, MT * P])
        w2 = sb("w2", [P, MT, C])
        wp = sb("wp", [P, 2, C])
        bst = sb("bst", [P, 2, 6])
        mv = sb("mv", [P, 2, 2])
        veps = sb("veps", [P, 2])
        rstd = sb("rstd", [P, 2])
        shift0 = sb("shift0", [P, 2])
        mhalf = sb("mhalf", [P, 1])
        table = sb("table", [P, 1])
        h1 = sb("h1", [P, C])
        h2 = sb("h2", [P, C])
        h1m = sb("h1m", [P, 2, C])
        hf = sb("hf", [P, 2, C])
        HS = sb("HS", [P, 2, 3 * P], F32R)
        HT = sb("HT", [P, 3, T], F32R)
        HTM = sb("HTM", [P, NG, 3, GB * T], F32R)
        QK = sb("QK", [P, 3, 2, H * HP], F32R)
        V = sb("V", [P, 4, H * HP])
        KT = sb("KT", [P, 2, G * T], F32R)
        Q1T = sb("Q1T", [P, 2, G * T], F32R)
        Q2T = sb("Q2T", [P, G * T], F32R)
        KBD = sb("KBD", [P, 3, G, 4 * T], F32R)
        nm = sb("nm", [P, H])
        Pr = sb("Pr", [P, H * T])
        OT = sb("OT", [P, G * T])
        rs = sb("rs", [P, H])
        o = sb("o", [P, 2 * P])
        oT = sb("oT", [P, 2, T])
        tmp = sb("tmp", [P, 2, C])
        tmp2 = sb("tmp2", [P, 2, C])
        GE = sb("GE", [P, NG, MT, GB * T])

        S1 = ctx.enter_context(nc.psum_tensor("S1", [P, 2 * BANK], F32))
        S2 = ctx.enter_context(nc.psum_tensor("S2", [P, 2 * BANK], F32))
        b4, b5, b6, b7 = (ctx.enter_context(nc.psum_tensor(f"bank{i}", [P, BANK], F32)) for i in (4, 5, 6, 7))
        fc1_bank = [S1[:, 0:BANK], S1[:, BANK:], S2[:, 0:BANK], S2[:, BANK:]]
        ada_bank = [fc1_bank[0], b5]
        ada_dram = nc.dram_tensor("ada_scratch", (L, HP, ADA), F32, kind="Internal").ap()

        x_in = [sem("x_first_in"), sem("x_rest_in")]
        const_in = sem("const_in")
        cond_in = sem("cond_in")
        wada_in = [sem(f"wada{i}_in") for i in range(2 * L)]
        wada_rest_in = [sem(f"wada{i}_rest_in") for i in range(L)]
        raw_q_in = sem("raw_q_in")
        raw_1_in = sem("raw_1_in")
        w2_in = sem("w2_in")
        wp_in = sem("wp_in")
        mod1_first = sem("mod1_first")
        mod1_first_mm = sem("mod1_first_mm")
        mod1_in = [sem(f"mod1_{b}_in") for b in (0, 2, 4)]
        mod2_in = [sem(f"mod2_{i}_in") for i in range(B // 2)]
        kbd_in = [sem(f"kbd{i}_in") for i in range(3)]
        out_done = sem("out_done")
        ada_out = [sem(f"ada{i}_out") for i in range(L)]
        dve_step = sem("dve_step")
        pool_step = sem("pool_step")
        cleared = sem("cleared")
        pool_cleared = sem("pool_cleared")
        dve_cleared = sem("dve_cleared")
        silu_e = sem("silu_e")
        silu_done = sem("silu_done")
        ident_ready = sem("ident_ready")
        ada_mm = sem("ada_mm")
        ada_ready = sem("ada_ready")
        masked = sem("masked")
        wq_hi = sem("wq_hi")
        wq_ready = sem("wq_ready")
        w1_hi = sem("w1_hi")
        w1_ready = sem("w1_ready")
        stats_done = sem("stats_done")
        scaled = sem("scaled")
        rstd_done = sem("rstd_done")
        h_ready = sem("h_ready")
        hs_hi = sem("hs_hi")
        hs_lo = sem("hs_lo")
        t1_done = sem("t1_done")
        ht_evac = sem("ht_evac")
        qkv_done = sem("qkv_done")
        split_done = sem("split_done")
        lo_done = sem("lo_done")
        tk_done = sem("tk_done")
        tq_done = sem("tq_done")
        kt_evac = sem("kt_evac")
        q1_evac = sem("q1_evac")
        s1_done = [sem("s1a_done"), sem("s1b_done")]
        max_done = [sem("maxa_done"), sem("maxb_done")]
        nm_done = sem("nm_done")
        t3_done = sem("t3_done")
        q2_evac = sem("q2_evac")
        s2_done = [sem("s2a_done"), sem("s2b_done")]
        exp_done = [sem("expa_done"), sem("expb_done")]
        pv_done = [sem("pva_done"), sem("pvb_done")]
        ot_evac = sem("ot_evac")
        t4_done = sem("t4_done")
        norm_done = sem("norm_done")
        t5_done = sem("t5_done")
        o_evac = sem("o_evac")
        proj_done = sem("proj_done")
        mul_done = sem("mul_done")
        x1_done = sem("x1_done")
        fc1_done = sem("fc1_done")
        gelu_done = sem("gelu_done")
        fc2_done = sem("fc2_done")
        mul2_done = sem("mul2_done")
        x2_done = sem("x2_done")

        def fc2_bank(l, b):
            return b7 if l == L - 1 and b % 2 else b4

        def s1_bank(b, half):
            return S2 if b == 0 and half == 1 else S1

        def heads(ap):
            return ap.rearrange("p (h r) -> p h r", r=HP)

        FIRST, LAST = -3, B + 1

        def norms(i):
            if i < B - 4:
                return [i + 3]
            return {B - 4: [B - 1, B], B: [i + 4, i + 5], B + 1: [i + 5]}.get(i, [i + 4])

        def split_norms(i):
            return (norms(i), []) if i == B else (norms(i)[0:1], norms(i)[1:])

        def transposes(i):
            return norms(i - 1) if i > FIRST else []

        block = ctx.enter_context(nc.Block())

        @block.sync
        def _(sp):
            def load(to, frm, s):
                sp.dma_start(to, frm).then_inc(s, 16)

            def load_split(raw, w, l, n, s):
                load(raw[:, 0, 0:n], w[l, 0:P, :], s)
                load(raw[0:w.shape[1] - P, 1, 0:n], w[l, P:, :], s)

            def load_ada(l, half):
                cols = slice(half * 3 * C, (half + 1) * 3 * C)
                load(wada[:, l, 0, cols], w_ada[l, 0:P, cols], wada_in[2 * l + half])

            def store_ada(l):
                sp.wait_ge(ada_ready, l + 1)
                load(ada_dram[l, :, :].rearrange("b (g c) -> g b c", g=4), ada[:, l, :], ada_out[l])

            def load_mods(mod, l, b0, b1, half, s):
                load(mod[:, b0:b1, :],
                     ada_dram[l, b0:b1, half * 3 * C:(half + 1) * 3 * C].partition_broadcast(P), s)

            def load_qkv(l):
                if l > 0:
                    sp.wait_ge(wq_ready, l)
                load_split(raw_q, w_qkv, l, 3 * C, raw_q_in)

            def load_proj(l):
                if l > 0:
                    sp.wait_ge(proj_done, B * l)
                load(wp[:, 0, :], w_proj[l, 0:P, :], wp_in)
                load(wp[0:R + 1, 1, :], w_proj[l, P:C + 1, :], wp_in)

            def load_fc1(l):
                if l > 0:
                    sp.wait_ge(w1_ready, l)
                load_split(raw_1, w_fc1, l, F, raw_1_in)

            def load_fc2(l):
                if l > 0:
                    sp.wait_ge(fc2_done, B * l)
                load(w2[:, 0:MT - 1, :], w_fc2[l, 0:(MT - 1) * P, :].rearrange("(m p) c -> p m c", p=P), w2_in)
                load(w2[0:FR + 1, MT - 1, :], w_fc2[l, (MT - 1) * P:F + 1, :], w2_in)

            def load_mod1(l):
                sp.wait_ge(ada_out[l], 16)
                if l > 0:
                    sp.wait_ge(mul_done, B * (l - 1) + GB)
                for k, (b0, b1) in enumerate(((0, 2), (2, 4), (4, B))):
                    if l == 0 and k == 0:
                        continue
                    if l > 0 and b1 == B:
                        sp.wait_ge(mul_done, B * l)
                    load_mods(MOD1, l, b0, b1, 0, mod1_in[k])

            def load_mod2(l, pair):
                if l > 0 and pair == 0:
                    sp.wait_ge(mul2_done, B * l)
                load_mods(MOD2, l, 2 * pair, 2 * pair + 2, 1, mod2_in[pair])

            load_ada(0, 0)
            sp.wait_ge(cleared, 1)
            load(cT[:, 0, :], cond_t[0:P, :], cond_in)
            load(cT[0:R, 1, :], cond_t[P:C, :], cond_in)
            load(wada[0:R + 2, 0, 1, :], w_ada[0, P:, :], wada_rest_in[0])
            load_ada(0, 1)
            load(X[:, 0, :], x[0, :, :], x_in[0])
            sp.wait_ge(cleared, 2)
            load_qkv(0)
            load(consts[:], marks, const_in)
            load(wada[0:R + 2, 1, 1, :], w_ada[1, P:, :], wada_rest_in[1])
            for half in range(2):
                load_ada(1, half)
            load(X[:, 1:B, :], x[1:B, :, :].rearrange("b t c -> t b c"), x_in[1])
            store_ada(0)
            load_mod1(0)
            sp.wait_ge(cleared, 3)
            load_fc1(0)
            load_proj(0)

            def move_k(n):
                if n < 3:
                    sp.wait_ge(pool_cleared, n + 2)
                sp.wait_ge(kt_evac, n + 1)
                if n >= 3:
                    sp.wait_ge(s2_done[1], n - 2)
                for j in range(4):
                    r = slice(HP * j, HP * (j + 1))
                    load(KBD[r, n % 3, :, j * T:(j + 1) * T].bitcast(F32),
                         KT[r, n % 2, :].rearrange("p (g t) -> p g t", g=G).bitcast(F32), kbd_in[n % 3])

            for l in range(L):
                for b in range(B):
                    move_k(B * l + b)
                    if b == 2:
                        load_fc2(l)
                    if b >= 3 and b - 3 < B // 2:
                        load_mod2(l, b - 3)
                    if b == 5 and l + 1 < L:
                        load_qkv(l + 1)
                if l + 1 < L:
                    store_ada(l + 1)
                    load_mod1(l + 1)
                    load_fc1(l + 1)
                    load_proj(l + 1)
            for b in range(B):
                sp.wait_ge(x2_done, B * (L - 1) + b + 1)
                load(out[b, :, :], X[:, b, :], out_done)
            sp.wait_ge(out_done, 16 * B)

        @block.gpsimd
        def _(pool):
            steps, masks = [0], [0]

            def link(ins):
                steps[0] += 1
                ins.then_inc(pool_step, 1)
                pool.wait_ge(pool_step, steps[0])

            def low_weights(l, part, raw, w, n, hi, ready):
                if part == 0:
                    pool.wait_ge(hi, 2 * l + 1)
                    nc.gpsimd.tensor_scalar(split_lo[:, 0:n], split_hi[:, 0:n].bitcast(F32), low_row, 1.0,
                                            ALU.mult, ALU.mult).then_inc(masked, 1)
                elif part == 1:
                    masks[0] += 1
                    pool.wait_ge(masked, masks[0])
                    nc.gpsimd.tensor_tensor(w[:, 2, 0:n], raw[:, 1, 0:n], split_lo[:, 0:n], ALU.subtract)
                else:
                    pool.wait_ge(hi, 2 * l + 2)
                    nc.gpsimd.tensor_tensor(w[:, 1, 0:n], raw[:, 0, 0:n], w[:, 0, 0:n].bitcast(F32),
                                            ALU.subtract).then_inc(ready, 1)

            def inv_std(q):
                pool.wait_ge(stats_done, q + 1)
                link(nc.gpsimd.tensor_scalar(veps[:, q % 2:q % 2 + 1], mv[:, q % 2, 1:2], 1.0, EPS, ALU.mult, ALU.add))
                nc.gpsimd.tensor_tensor(rstd[:, q % 2:q % 2 + 1], veps[:, q % 2:q % 2 + 1], mhalf[:],
                                        ALU.pow).then_inc(rstd_done, 1)

            def modulate(q, l, b):
                k = slice(q % 2, q % 2 + 1)
                pool.wait_ge(rstd_done, q + 1)
                link(nc.gpsimd.tensor_scalar(shift0[:, k], mv[:, q % 2, 0:1], rstd[:, k], -1.0, ALU.mult, ALU.mult))
                link(nc.gpsimd.tensor_scalar(h1[:], X[:, b, :], rstd[:, k], shift0[:, k], ALU.mult, ALU.add))
                if l == 0 and b < 2:
                    pool.wait_ge(mod1_first, b + 1)
                else:
                    pool.wait_ge(mod1_in[min(b // 2, 2)], 16 * l if b < 2 else 16 * (l + 1))
                link(nc.gpsimd.tensor_tensor(h2[:], h1[:], MOD1[:, b, C:2 * C], ALU.mult))
                nc.gpsimd.tensor_tensor(hf[:, q % 2, :], h2[:], MOD1[:, b, 0:C], ALU.add).then_inc(h_ready, 1)

            def low_part(q):
                hs, h = HS[:, q % 2, :], hf[:, q % 2, :]
                pool.wait_ge(hs_hi, q + 1)
                nc.gpsimd.tensor_tensor(hs[:, LO_A:LO_A + P], h[:, 0:P], hs[:, 0:P].bitcast(F32), ALU.subtract)
                nc.gpsimd.tensor_tensor(hs[:, LO_R:LO_R + R], h[:, P:C], hs[:, P:C].bitcast(F32), ALU.subtract)
                nc.gpsimd.tensor_copy(hs[:, HI_R:HI_R + R], hs[:, P:C].bitcast(F32)).then_inc(hs_lo, 1)

            def add_residual(n, b):
                pool.wait_ge(mul_done, n + 1)
                nc.gpsimd.tensor_tensor(X[:, b, :], X[:, b, :], tmp[:, n % 2, :], ALU.add).then_inc(x1_done, 1)

            def slot(l, i):
                q0, n = 2 * B * l, B * l + i
                for q in norms(i):
                    inv_std(q0 + q)
                for q in norms(i):
                    if q < B:
                        modulate(q0 + q, l, q)
                if 2 <= i < 5:
                    low_weights(l, i - 2, raw_1, w1, MT * P, w1_hi, w1_ready)
                if 6 <= i < 9 and l + 1 < L:
                    low_weights(l + 1, i - 6, raw_q, wq, 3 * C, wq_hi, wq_ready)
                for q in norms(i):
                    low_part(q0 + q)
                if 0 <= i - 2 < B:
                    add_residual(n - 2, i - 2)

            nc.gpsimd.memset(mhalf[:], -0.5)
            link(nc.gpsimd.memset(V[:], 0.0))
            nc.gpsimd.memset(V[:].rearrange("p a (h r) -> p (a h) r", r=HP)[:, :, D:D + 1], 1.0)
            nc.gpsimd.memset(GE[:, :, MT - 1, :], 1.0)
            nc.gpsimd.memset(KBD[:, 0, :, :].bitcast(F32), 0.0).then_inc(pool_cleared, 2)
            inv_std(0)
            nc.gpsimd.memset(KBD[:, 1, :, :].bitcast(F32), 0.0).then_inc(pool_cleared, 1)
            low_part(0)
            slot(0, FIRST + 1)
            nc.gpsimd.memset(KBD[:, 2, :, :].bitcast(F32), 0.0).then_inc(pool_cleared, 1)
            pool.wait_ge(const_in, 16)
            for l in range(L):
                for i in range(-1 if l == 0 else 0, LAST + 1):
                    slot(l, i)
                inv_std(2 * B * (l + 1) - 1)
                if l + 1 < L:
                    for i in range(FIRST, 0):
                        slot(l + 1, i)

        @block.scalar
        def _(act):
            def high_weights(part, l, raw, w, n, arrived, hi):
                if part == 0:
                    act.wait_ge(arrived, 32 * (l + 1))
                    nc.scalar.copy(split_hi[:, 0:n], raw[:, 1, 0:n]).then_inc(hi, 1)
                else:
                    nc.scalar.copy(w[:, 0, 0:n], raw[:, 0, 0:n]).then_inc(hi, 1)

            def high_part(q):
                act.wait_ge(h_ready, q + 1)
                if q >= 2:
                    act.wait_ge(t1_done, q - 1)
                nc.scalar.copy(HS[:, q % 2, 0:C], hf[:, q % 2, :]).then_inc(hs_hi, 1)

            def evac_ht(q, n):
                act.wait_ge(t1_done, q + 1)
                if n > 0:
                    act.wait_ge(qkv_done, n)
                nc.scalar.copy(HT[:].rearrange("p k t -> p (k t)"), b5[:, 0:3 * T]).then_inc(ht_evac, 1)

            def split_qkv(n):
                act.wait_ge(qkv_done, n + 1)
                if n >= 3:
                    act.wait_ge(t3_done, n - 2)
                if n >= 4:
                    act.wait_ge(pv_done[1], n - 3)
                for k, slot in ((0, 0), (1, D)):
                    src = b5[:, k * C:(k + 1) * C].rearrange("p (h d) -> p h d", d=D)
                    dst = heads(QK[:, n % 3, k, :])[:, :, slot:slot + 2 * D].rearrange("p h (s d) -> p h s d", d=D)
                    nc.scalar.copy(dst, src.unsqueeze(2).broadcast_to([P, H, 2, D]))
                nc.scalar.copy(heads(V[:, n % 4, :])[:, :, 0:D],
                               b5[:, 2 * C:3 * C].rearrange("p (h d) -> p h d", d=D)).then_inc(split_done, 1)

            def evac_q1(n):
                act.wait_ge(tq_done, n + 1)
                if n >= 2:
                    act.wait_ge(s1_done[1], n - 1)
                nc.scalar.copy(Q1T[:, n % 2, :], b7[:]).then_inc(q1_evac, 1)

            def evac_q2(n):
                act.wait_ge(t3_done, n + 1)
                if n > 0:
                    act.wait_ge(s2_done[1], n)
                nc.scalar.copy(Q2T[:], b6[:]).then_inc(q2_evac, 1)

            def exp_half(n, half):
                act.wait_ge(s2_done[half], n + 1)
                if n > 0:
                    act.wait_ge(pv_done[half], n)
                nc.scalar.activation(Pr[:, half * HALF:(half + 1) * HALF], S2[:], ACT.Exp,
                                     scale=SCALE).then_inc(exp_done[half], 1)

            def evac_ot(n):
                act.wait_ge(pv_done[1], n + 1)
                if n > 0:
                    act.wait_ge(t4_done, n)
                nc.scalar.copy(OT[:], b7[:]).then_inc(ot_evac, 1)

            def evac_o(n):
                act.wait_ge(t5_done, n + 1)
                if n > 0:
                    act.wait_ge(proj_done, n)
                nc.scalar.copy(oT[:].rearrange("p k t -> p (k t)"), b4[:, 0:2 * T]).then_inc(o_evac, 1)

            def evac_htm(q, n):
                act.wait_ge(t1_done, q + 1)
                gg, g, c = n // GB, n // GB % NG, n % GB * T
                if gg >= NG:
                    act.wait_ge(fc1_done, MT * (gg - 1))
                nc.scalar.copy(HTM[:, g, :, c:c + T],
                               b5[:, 0:3 * T].rearrange("p (k t) -> p k t", k=3)).then_inc(ht_evac, 1)

            def gelu(gg, g, m):
                act.wait_ge(fc1_done, MT * gg + m + 1)
                if gg >= NG:
                    act.wait_ge(fc2_done, GB * (gg - 1))
                rows = P if m < MT - 1 else FR
                nc.scalar.activation(GE[0:rows, g, m, :], fc1_bank[(MT * g + m) % 4][0:rows, :],
                                     ACT.Gelu_apprx_tanh).then_inc(gelu_done, 1)

            def finish_ada(l):
                act.wait_ge(ada_mm, l + 1)
                nc.scalar.copy(ada[:, l, :], ada_bank[l][:, 0:AC]).then_inc(ada_ready, 1)

            def slot(l, i):
                q0, n0 = 2 * B * l, B * l
                for q in transposes(i)[0:1]:
                    if q < B:
                        evac_ht(q0 + q, n0 + q)
                    else:
                        evac_htm(q0 + q, n0 + q - B)
                if i == LAST:
                    nc.scalar.activation(table[:], mhalf[:], ACT.Gelu_apprx_tanh)
                if l == 0 and i == -2:
                    act.wait_ge(mod1_first_mm, 2)
                    nc.scalar.copy(MOD1[:, 1, :], b7[:, 0:3 * C]).then_inc(mod1_first, 1)
                if 0 <= i + 1 < B:
                    evac_q1(n0 + i + 1)
                if i in (1, 2):
                    high_weights(i - 1, l, raw_1, w1, MT * P, raw_1_in, w1_hi)
                if i in (6, 7) and l + 1 < L:
                    if i == 6:
                        act.wait_ge(qkv_done, n0 + B)
                    high_weights(i - 6, l + 1, raw_q, wq, 3 * C, raw_q_in, wq_hi)
                if 0 <= i - 1 < B:
                    exp_half(n0 + i - 1, 0)
                if 0 <= i + 2 < B:
                    split_qkv(n0 + i + 2)
                if l + 1 < L and i == B - 1:
                    finish_ada(l + 1)
                if 0 <= i - 2 < B:
                    evac_o(n0 + i - 2)
                for q in split_norms(i)[0]:
                    high_part(q0 + q)
                if i == 0:
                    nc.scalar.activation(table[:], mhalf[:], ACT.Exp)
                if 0 <= i - 1 < B:
                    exp_half(n0 + i - 1, 1)
                if 0 <= i < B:
                    evac_q2(n0 + i)
                if 0 <= i - 1 < B:
                    evac_ot(n0 + i - 1)
                for q in split_norms(i)[1]:
                    high_part(q0 + q)
                for q in transposes(i)[1:]:
                    evac_htm(q0 + q, n0 + q - B)
                if i == LAST:
                    for m in range(3):
                        gelu(NG * l, 0, m)

            act.wait_ge(cond_in, 32)
            nc.scalar.activation(ce[:], cT[:], ACT.Exp, scale=-1.0).then_inc(silu_e, 1)
            for part in range(2):
                high_weights(part, 0, raw_q, wq, 3 * C, raw_q_in, wq_hi)
            act.wait_ge(mod1_first_mm, 1)
            nc.scalar.copy(MOD1[:, 0, :], b6[:, 0:3 * C]).then_inc(mod1_first, 1)
            act.wait_ge(dve_cleared, 1)
            slot(0, FIRST)
            finish_ada(0)
            act.wait_ge(dve_cleared, 2)
            act.wait_ge(pool_cleared, 1)
            for i in (-2, -1):
                slot(0, i)
            for l in range(L):
                for i in range(LAST + 1):
                    slot(l, i)
                q0, n0 = 2 * B * l + B, B * l
                gelu(NG * l, 0, 3)
                high_part(q0 + B - 1)
                gelu(NG * l, 0, 4)
                evac_htm(q0 + B - 2, n0 + B - 2)
                evac_htm(q0 + B - 1, n0 + B - 1)
                for m in range(MT):
                    gelu(NG * l + 1, 1, m)
                    if l + 1 < L and m - 3 in range(FIRST, 0):
                        slot(l + 1, m - 3)

        @block.vector
        def _(dve):
            steps = [0]

            def link(ins):
                steps[0] += 1
                ins.then_inc(dve_step, 1)
                dve.wait_ge(dve_step, steps[0])

            def norm_stats(q, b):
                if q >= 2:
                    dve.wait_ge(h_ready, q - 1)
                link(nc.vector.bn_stats(bst[:, q % 2, :], X[:, b, :]))
                nc.vector.bn_aggr(mv[:, q % 2, :], bst[:, q % 2, :]).then_inc(stats_done, 1)

            def scale_mlp(q, l, b):
                dve.wait_ge(stats_done, q + 1)
                dve.wait_ge(mod2_in[b // 2], 16 * (l + 1))
                nc.vector.scalar_tensor_tensor(out=h1m[:, q % 2, :], in0=X[:, b, :], scalar=mv[:, q % 2, 0:1],
                                               in1=MOD2[:, b, C:2 * C],
                                               op0=ALU.subtract, op1=ALU.mult).then_inc(scaled, 1)

            def shift_mlp(q, l, b):
                dve.wait_ge(scaled, B * l + b + 1)
                dve.wait_ge(rstd_done, q + 1)
                dve.wait_ge(h_ready, q)
                dve.wait_ge(hs_lo, q - 1)
                nc.vector.scalar_tensor_tensor(out=hf[:, q % 2, :], in0=h1m[:, q % 2, :], scalar=rstd[:, q % 2:q % 2 + 1],
                                               in1=MOD2[:, b, 0:C],
                                               op0=ALU.mult, op1=ALU.add).then_inc(h_ready, 1)

            def modulate_first():
                dve.wait_ge(stats_done, 1)
                dve.wait_ge(mod1_first, 1)
                link(nc.vector.scalar_tensor_tensor(out=h1m[:, 0, :], in0=X[:, 0, :], scalar=mv[:, 0, 0:1],
                                                    in1=MOD1[:, 0, C:2 * C],
                                                    op0=ALU.subtract, op1=ALU.mult))
                dve.wait_ge(rstd_done, 1)
                nc.vector.scalar_tensor_tensor(out=hf[:, 0, :], in0=h1m[:, 0, :], scalar=rstd[:, 0:1],
                                               in1=MOD1[:, 0, 0:C],
                                               op0=ALU.mult, op1=ALU.add).then_inc(h_ready, 1)

            def low_part(q):
                hs, h = HS[:, q % 2, :], hf[:, q % 2, :]
                dve.wait_ge(hs_hi, q + 1)
                dve.wait_ge(hs_lo, q)
                nc.vector.tensor_tensor(hs[:, LO_A:LO_A + P], h[:, 0:P], hs[:, 0:P].bitcast(F32), ALU.subtract)
                nc.vector.tensor_tensor(hs[:, LO_R:LO_R + R], h[:, P:C], hs[:, P:C].bitcast(F32), ALU.subtract)
                nc.vector.tensor_copy(hs[:, HI_R:HI_R + R], hs[:, P:C].bitcast(F32)).then_inc(hs_lo, 1)

            def low_weights_first():
                n = 3 * C
                dve.wait_ge(wq_hi, 2)
                link(nc.vector.tensor_scalar(split_lo[:, 0:n], split_hi[:, 0:n].bitcast(F32), low_row, 1.0,
                                             ALU.mult, ALU.mult))
                nc.vector.tensor_tensor(wq[:, 2, :], raw_q[:, 1, :], split_lo[:, 0:n], ALU.subtract)
                nc.vector.tensor_tensor(wq[:, 1, :], raw_q[:, 0, :], wq[:, 0, :].bitcast(F32),
                                        ALU.subtract).then_inc(wq_ready, 1)

            def low_qk(n):
                dve.wait_ge(split_done, n + 1)
                for k, slot in ((0, 2 * D), (1, 0)):
                    v = heads(QK[:, n % 3, k, :])
                    nc.vector.tensor_tensor(v[:, :, slot:slot + D],
                                            b5[:, k * C:(k + 1) * C].rearrange("p (h d) -> p h d", d=D),
                                            v[:, :, D:2 * D].bitcast(F32), ALU.subtract)
                nc.vector.memset(heads(QK[:, n % 3, 0, :])[:, :, MAX_HI:MAX_LO + 1].bitcast(F32),
                                 0.0).then_inc(lo_done, 1)

            def evac_kt(n):
                dve.wait_ge(tk_done, n + 1)
                if n >= 2:
                    dve.wait_ge(kbd_in[(n - 2) % 3], 64 * ((n - 2) // 3 + 1))
                nc.vector.tensor_copy(KT[:, n % 2, :], b6[:]).then_inc(kt_evac, 1)

            def neg_max(b, n, half):
                dve.wait_ge(s1_done[half], n + 1)
                nc.vector.tensor_reduce(nm[:, half * H // 2:(half + 1) * H // 2],
                                        s1_bank(b, half)[:].rearrange("p (h t) -> p h t", t=T), AX.X, ALU.max,
                                        negate=True).then_inc(max_done[half], 1)

            def split_max(n):
                v = heads(QK[:, n % 3, 0, :])
                m = nm[:].unsqueeze(2)
                dve.wait_ge(max_done[1], n + 1)
                link(nc.vector.tensor_copy(v[:, :, MAX_HI:MAX_HI + 1], m))
                nc.vector.tensor_tensor(v[:, :, MAX_LO:MAX_LO + 1], m, v[:, :, MAX_HI:MAX_HI + 1].bitcast(F32),
                                        ALU.subtract).then_inc(nm_done, 1)

            def normalise(n):
                v = heads(b4[:])
                dve.wait_ge(t4_done, n + 1)
                link(nc.vector.reciprocal(rs[:].unsqueeze(2), v[:, :, D:D + 1]))
                if n > 0:
                    dve.wait_ge(t5_done, n)
                nc.vector.tensor_tensor(o[:, 0:C].rearrange("p (h d) -> p h d", d=D), v[:, :, 0:D],
                                        rs[:].unsqueeze(2).broadcast_to([P, H, D]), ALU.mult).then_inc(norm_done, 1)

            def gate(n, b):
                dve.wait_ge(proj_done, n + 1)
                if n >= 2:
                    dve.wait_ge(x1_done, n - 1)
                nc.vector.tensor_tensor(tmp[:, n % 2, :], b4[:, 2 * T:2 * T + C], MOD1[:, b, 2 * C:3 * C],
                                        ALU.mult).then_inc(mul_done, 1)

            def residual2(l, b):
                n = B * l + b
                dve.wait_ge(fc2_done, n + 1)
                nc.vector.tensor_tensor(tmp2[:, n % 2, :], fc2_bank(l, b)[:, 0:C], MOD2[:, b, 2 * C:3 * C],
                                        ALU.mult).then_inc(mul2_done, 1)
                dve.wait_ge(mul2_done, n + 1)
                nc.vector.tensor_tensor(X[:, b, :], X[:, b, :], tmp2[:, n % 2, :], ALU.add).then_inc(x2_done, 1)

            def stats(l, q):
                n = B * l
                if q >= B:
                    dve.wait_ge(x1_done, n + q - B + 1)
                elif l == 0:
                    dve.wait_ge(x_in[min(q, 1)], 16)
                else:
                    dve.wait_ge(x2_done, n - B + q + 1)
                norm_stats(2 * B * l + q, q % B)

            def slot(l, i):
                q0, n = 2 * B * l, B * l + i
                if l > 0 and i < 0:
                    residual2(l - 1, i + 4)
                if 0 <= i + 1 < B:
                    evac_kt(n + 1)
                if 0 <= i < B:
                    neg_max(i, n, 0)
                if l > 0 and i == 1:
                    residual2(l - 1, GB + 2)
                if 0 <= i - 2 < B:
                    normalise(n - 2)
                for q in split_norms(i)[0]:
                    if q >= B:
                        scale_mlp(q0 + q, l, q - B)
                        shift_mlp(q0 + q, l, q - B)
                if 0 <= i < B:
                    neg_max(i, n, 1)
                    split_max(n)
                if l > 0 and i == 0:
                    residual2(l - 1, GB)
                if 0 <= i + 2 < B:
                    low_qk(n + 2)
                if l > 0 and i in (0, 1):
                    residual2(l - 1, GB + 2 * i + 1)
                for q in split_norms(i)[1]:
                    scale_mlp(q0 + q, l, q - B)
                    shift_mlp(q0 + q, l, q - B)
                if 0 <= i - 2 < B:
                    gate(n - 2, i - 2)
                for q in norms(i + 1) if i < LAST else [2 * B - 1]:
                    stats(l, q)

            nc.vector.memset(cT[:], 0.0).then_inc(cleared, 1)
            nc.vector.memset(raw_q[:, 1, :], 0.0).then_inc(cleared, 1)
            nc.vector.memset(cs[:, 0, :], 0.0)
            nc.vector.memset(cs[:, 1, :], 1.0)
            nc.vector.memset(raw_1[:], 0.0).then_inc(cleared, 1)
            link(nc.vector.memset(HS[:].bitcast(F32), 0.0))
            nc.vector.memset(HS[:, :, ONES:ONES + 2].bitcast(F32), 1.0).then_inc(dve_cleared, 1)
            dve.wait_ge(cond_in, 32)
            dve.wait_ge(silu_e, 1)
            link(nc.vector.tensor_scalar_add(ce[:], ce[:], 1.0))
            link(nc.vector.reciprocal(cr[:], ce[:]))
            for r, k in ((P, 0), (R, 1)):
                last = nc.vector.tensor_tensor(cs[0:r, k, 0:B], cT[0:r, k, :], cr[0:r, k, :], ALU.mult)
            last.then_inc(silu_done, 1)
            nc.vector.memset(QK[:, :, 0, :].bitcast(F32), 0.0)
            stats(0, 0)
            link(nc.vector.memset(QK[:, :, 1, :].bitcast(F32), 0.0))
            for third in range(3):
                last = nc.vector.memset(heads(QK[:, third, 1, :])[:, :, MAX_HI:MAX_LO + 1].bitcast(F32), 1.0)
            last.then_inc(dve_cleared, 1)
            modulate_first()
            dve.wait_ge(const_in, 16)
            nc.vector.tensor_copy(ident_r[:], ident).then_inc(ident_ready, 1)
            low_weights_first()
            link(nc.vector.memset(o[:], 0.0))
            nc.vector.memset(o[:, C:C + 1], 1.0)
            for l in range(L):
                for i in range(FIRST if l == 0 else 0, LAST + 1):
                    slot(l, i)
                scale_mlp(2 * B * (l + 1) - 1, l, B - 1)
                shift_mlp(2 * B * (l + 1) - 1, l, B - 1)
                low_part(2 * B * (l + 1) - 1)
                if l + 1 < L:
                    residual2(l, 0)
                    stats(l + 1, 0)
                    for i in range(FIRST, 0):
                        slot(l + 1, i)
                else:
                    for b in range(B):
                        residual2(l, b)

        @block.tensor
        def _(pe):
            def transpose_h(q):
                pe.wait_ge(hs_lo, q + 1)
                for k in range(3):
                    last = nc.tensor.transpose(b5[:, k * T:(k + 1) * T].bitcast(F32R),
                                               HS[:, q % 2, k * P:(k + 1) * P], ident_r[:])
                last.then_inc(t1_done, 1)

            def qkv(l, b, q, n):
                if b == 0:
                    pe.wait_ge(wq_ready, l + 1)
                pe.wait_ge(ht_evac, q + 1)
                pairs = ((0, 0), (0, 1), (1, 2), (2, 0))
                for k, (h, w) in enumerate(pairs):
                    last = nc.tensor.matmul(b5[:, 0:3 * C], HT[:, h, :], wq[:, w, :], start=(k == 0), stop=(k == 3))
                last.then_inc(qkv_done, 1)

            def transpose_k(l, b, n):
                pe.wait_ge(lo_done, n + 1)
                if b >= 2:
                    pe.wait_ge(q2_evac, n - 1)
                if b == 1:
                    pe.wait_ge(kt_evac, n)
                if b == 0 and l == 0:
                    pe.wait_ge(mod1_first, 1)
                for g in range(G):
                    last = nc.tensor.transpose(b6[:, g * T:(g + 1) * T].bitcast(F32R),
                                               QK[:, n % 3, 1, g * P:(g + 1) * P], ident_r[:])
                last.then_inc(tk_done, 1)

            def transpose_q(b, n):
                if b >= 3:
                    pe.wait_ge(ot_evac, n - 2)
                elif b > 0:
                    pe.wait_ge(q1_evac, n)
                for g in range(G):
                    last = nc.tensor.transpose(b7[:, g * T:(g + 1) * T].bitcast(F32R),
                                               QK[:, n % 3, 0, g * P:(g + 1) * P], ident_r[:])
                last.then_inc(tq_done, 1)

            def scores_for_max(b, n, half):
                if n == 0 and half == 0:
                    pe.wait_ge(ada_ready, 1)
                elif b == 0 and half == 0:
                    pe.wait_ge(gelu_done, MT * NG * (n // B))
                if half == 0:
                    pe.wait_ge(kbd_in[n % 3], 64 * (n // 3 + 1))
                    pe.wait_ge(q1_evac, n + 1)
                    if n > 0:
                        pe.wait_ge(max_done[1], n)
                elif b > 0:
                    pe.wait_ge(max_done[0], n + 1)
                for k in range(2):
                    g = 2 * half + k
                    last = nc.tensor.matmul(s1_bank(b, half)[:, k * BANK:(k + 1) * BANK], Q1T[:, n % 2, g * T:(g + 1) * T],
                                            KBD[:, n % 3, g, :], start=True, stop=True)
                last.then_inc(s1_done[half], 1)

            def transpose_q2(b, n):
                pe.wait_ge(nm_done, n + 1)
                pe.wait_ge(kt_evac, n + 2 if b + 1 < B else n + 1)
                for g in range(G):
                    last = nc.tensor.transpose(b6[:, g * T:(g + 1) * T].bitcast(F32R),
                                               QK[:, n % 3, 0, g * P:(g + 1) * P], ident_r[:])
                last.then_inc(t3_done, 1)

            def scores_less_max(b, n, half):
                if b == 0 and half == 0:
                    pe.wait_ge(max_done[1], n + 1)
                if half == 0:
                    pe.wait_ge(q2_evac, n + 1)
                    if n > 0:
                        pe.wait_ge(exp_done[1], n)
                else:
                    pe.wait_ge(exp_done[0], n + 1)
                for k in range(H // 2):
                    g, j = 2 * half + k // 4, k % 4
                    last = nc.tensor.matmul(S2[:, k * T:(k + 1) * T], KBD[:, n % 3, g, j * T:(j + 1) * T],
                                            Q2T[:, g * T:(g + 1) * T], start=True, stop=True)
                last.then_inc(s2_done[half], 1)

            def values(b, n, half):
                pe.wait_ge(exp_done[half], n + 1)
                if half == 0:
                    if b + 2 < B:
                        pe.wait_ge(q1_evac, n + 3)
                    elif n > 0:
                        pe.wait_ge(ot_evac, n)
                for h in range(half * H // 2, (half + 1) * H // 2):
                    g, j = h // 4, h % 4
                    last = nc.tensor.matmul(b7[HP * j:HP * (j + 1), g * T:(g + 1) * T],
                                            V[:, n % 4, HP * h:HP * (h + 1)], Pr[:, h * T:(h + 1) * T],
                                            start=True, stop=True)
                last.then_inc(pv_done[half], 1)

            def transpose_ot(l, b, n):
                pe.wait_ge(ot_evac, n + 1)
                if b > 0:
                    pe.wait_ge(mul_done, n)
                elif l > 0:
                    pe.wait_ge(mul2_done, n)
                for g in range(G):
                    last = nc.tensor.transpose(b4[:, g * T:(g + 1) * T], OT[:, g * T:(g + 1) * T], ident)
                last.then_inc(t4_done, 1)

            def transpose_o(n):
                pe.wait_ge(norm_done, n + 1)
                for k in range(2):
                    last = nc.tensor.transpose(b4[:, k * T:(k + 1) * T], o[:, k * P:(k + 1) * P], ident)
                last.then_inc(t5_done, 1)

            def project(l, b, n):
                pe.wait_ge(o_evac, n + 1)
                if b == 0:
                    pe.wait_ge(wp_in, 32 * (l + 1))
                for k, rows in enumerate((P, R + 1)):
                    last = nc.tensor.matmul(b4[:, 2 * T:2 * T + C], oT[0:rows, k, :], wp[0:rows, k, :],
                                            start=(k == 0), stop=(k == 1))
                last.then_inc(proj_done, 1)

            def fc1(l, g, m):
                k = MT * g + m
                if m == 0:
                    pe.wait_ge(ht_evac, 2 * B * l + B + GB * (g + 1))
                    pe.wait_ge(w1_ready, l + 1)
                if k >= 4:
                    pe.wait_ge(gelu_done, MT * NG * l + k - 3)
                elif k == 0:
                    pe.wait_ge(max_done[1], B * (l + 1))
                elif k == 2:
                    pe.wait_ge(exp_done[1], B * (l + 1))
                pairs = ((0, 0), (0, 2), (1, 0), (2, 1))
                for s, (w, h) in enumerate(pairs):
                    last = nc.tensor.matmul(fc1_bank[k % 4], w1[:, w, m * P:(m + 1) * P], HTM[:, g, h, :],
                                            start=(s == 0), stop=(s == 3))
                last.then_inc(fc1_done, 1)

            def fc2(l, b, n):
                g = b // GB
                if b == 0:
                    pe.wait_ge(w2_in, 32 * (l + 1))
                    pe.wait_ge(mul_done, n + B)
                elif l < L - 1:
                    pe.wait_ge(mul2_done, n)
                elif b >= 2:
                    pe.wait_ge(mul2_done, n - 1)
                c = (b % GB) * T
                for m in range(MT):
                    if b % GB == 0:
                        pe.wait_ge(gelu_done, MT * (NG * l + g) + m + 1)
                    rows = P if m < MT - 1 else FR + 1
                    last = nc.tensor.matmul(fc2_bank(l, b)[:, 0:C], GE[0:rows, g, m, c:c + T], w2[0:rows, m, :],
                                            start=(m == 0), stop=(m == MT - 1))
                last.then_inc(fc2_done, 1)

            def ada_columns(l):
                for half in range(2):
                    pe.wait_ge(wada_in[2 * l + half], 16)
                pe.wait_ge(wada_rest_in[l], 16)
                for k, rows in enumerate((P, R + 2)):
                    for g in range(4):
                        last = nc.tensor.matmul(ada_bank[l][HP * g:HP * (g + 1), 0:AC], cs[0:rows, k, :],
                                                wada[0:rows, l, k, AC * g:AC * (g + 1)],
                                                start=(k == 0), stop=(k == 1))
                last.then_inc(ada_mm, 1)

            def slot(l, i):
                q0, n = 2 * B * l, B * l + i
                if 0 <= i + 1 < B:
                    transpose_k(l, i + 1, n + 1)
                for q in transposes(i)[0:1]:
                    if 1 <= q <= B:
                        pe.wait_ge(lo_done, n - i + q)
                    elif q > 0 or l > 0:
                        pe.wait_ge(ht_evac, q0 + q)
                    if l + 1 < L and i == B:
                        pe.wait_ge(ada_ready, l + 2)
                    transpose_h(q0 + q)
                if 0 < i < B:
                    scores_for_max(i, n, 0)
                if 0 <= i + 1 < B:
                    transpose_q(i + 1, n + 1)
                if l > 0 and i in (-2, -1):
                    fc1(l - 1, 1, i + 4)
                if l == 0 and i == -2:
                    pe.wait_ge(ada_ready, 1)
                    for g in range(2):
                        row = HP * g + 1
                        last = nc.tensor.matmul(b7[:, AC * g:AC * (g + 1)], ident[:, row:row + 1].broadcast_to([P, P]),
                                                ada[:, 0, :], start=True, stop=True)
                    last.then_inc(mod1_first_mm, 1)
                if l > 0 and i == 1:
                    fc2(l - 1, GB + 2, n - 1 - B + GB + 2)
                if i == 0:
                    scores_for_max(i, n, 0)
                    scores_for_max(i, n, 1)
                if i <= 0 and 0 <= i + 2 < B:
                    qkv(l, i + 2, q0 + i + 2, n + 2)
                if l > 0 and i == 0:
                    fc2(l - 1, GB, n - B + GB)
                if i == B:
                    scores_less_max(i - 1, n - 1, 0)
                if i == LAST:
                    fc1(l, 0, 2)
                if 0 <= i - 2 < B:
                    transpose_ot(l, i - 2, n - 2)
                if 0 <= i - 1 < B - 1:
                    scores_less_max(i - 1, n - 1, 0)
                if 0 < i < B:
                    scores_for_max(i, n, 1)
                if i == B:
                    fc1(l, 0, 0)
                if i > 0 and 0 <= i + 2 < B:
                    qkv(l, i + 2, q0 + i + 2, n + 2)
                if l + 1 < L and i == B - 1:
                    pe.wait_ge(ht_evac, q0 + i + 4)
                    ada_columns(l + 1)
                if 0 <= i - 2 < B:
                    transpose_o(n - 2)
                if 0 <= i - 1 < B:
                    scores_less_max(i - 1, n - 1, 1)
                    values(i - 1, n - 1, 0)
                if 0 <= i < B:
                    transpose_q2(i, n)
                if l > 0 and i in (0, 1):
                    fc2(l - 1, GB + 2 * i + 1, n - i - B + GB + 2 * i + 1)
                if i >= B:
                    fc1(l, 0, 1 if i == B else 3)
                if 0 <= i - 2 < B:
                    project(l, i - 2, n - 2)
                for q in transposes(i)[1:]:
                    pe.wait_ge(lo_done, n - i + B)
                    pe.wait_ge(ht_evac, q0 + q)
                    transpose_h(q0 + q)
                if 0 <= i - 1 < B:
                    values(i - 1, n - 1, 1)

            pe.wait_ge(silu_done, 1)
            pe.wait_ge(wada_in[0], 16)
            pe.wait_ge(wada_rest_in[0], 16)
            for k, rows in enumerate((P, R + 2)):
                last = nc.tensor.matmul(b6[:, 0:3 * C], cs[0:rows, k, 0:1].broadcast_to([rows, P]),
                                        wada[0:rows, 0, k, 0:3 * C], start=(k == 0), stop=(k == 1))
            last.then_inc(mod1_first_mm, 1)
            ada_columns(0)
            pe.wait_ge(ident_ready, 1)
            slot(0, -2)
            slot(0, -1)
            for l in range(L):
                for i in range(LAST + 1):
                    slot(l, i)
                q0, n0 = 2 * B * l, B * l
                pe.wait_ge(ht_evac, q0 + 2 * B - 2)
                transpose_h(q0 + 2 * B - 2)
                fc1(l, 0, 4)
                fc2(l, 0, n0)
                pe.wait_ge(ht_evac, q0 + 2 * B - 1)
                transpose_h(q0 + 2 * B - 1)
                fc2(l, 1, n0 + 1)
                fc1(l, 1, 0)
                fc2(l, 2, n0 + 2)
                fc1(l, 1, 1)
                if l + 1 < L:
                    slot(l + 1, -2)
                    fc2(l, 3, n0 + 3)
                    slot(l + 1, -1)
                    fc1(l, 1, 4)
                else:
                    fc2(l, 3, n0 + 3)
                    for m in range(2, MT):
                        fc1(l, 1, m)
            for b in range(GB, B):
                fc2(L - 1, b, B * (L - 1) + b)


def kernel(**inputs):
    import numpy as np
    import concourse.bacc as bacc
    from concourse import mybir as mb
    from concourse.bass_utils import run_bass_kernel_spmd as run

    def by_layer(names, rows):
        return np.stack([np.concatenate(rows(np.asarray(inputs[w]), np.asarray(inputs[b])[None, :])) for w, b in names])

    def plain(w, b):
        return [w, b]

    def stacked(w, b):
        return [w, w[128:], w[128:], b, b]

    x = np.ascontiguousarray(inputs["x"])
    channels = x.shape[2]
    ones = np.zeros((1, 6 * channels), np.float32)
    for scale in (1, 4):
        ones[:, scale * channels:(scale + 1) * channels] = 1.0

    def with_ones(w, b):
        return [w, b, ones]

    rest = x.shape[2] - 128
    marks = np.zeros((128, 129), np.float32)
    marks[:, 0:128] = np.eye(128, dtype=np.float32)
    marks[2 * rest:3 * rest, 128] = 1.0
    marks[3 * rest + 1, 128] = 1.0
    arrays = {
        "x": x,
        "cond_t": np.ascontiguousarray(np.asarray(inputs["cond_1152"]).T),
        "w_ada": by_layer([("L0_cond_W_ada", "L0_cond_b_ada"), ("L1_cond_ada_w", "L1_cond_ada_b")], with_ones),
        "w_qkv": by_layer([("L0_cond_W_qkv", "L0_cond_b_qkv"), ("L1_cond_qkv_w", "L1_cond_qkv_b")], stacked),
        "w_proj": by_layer([("L0_cond_W_proj", "L0_cond_b_proj"), ("L1_cond_out_w", "L1_cond_out_b")], plain),
        "w_fc1": by_layer([("L0_cond_W_fc1", "L0_cond_b_fc1"), ("L1_cond_w1", "L1_cond_b1")], stacked),
        "w_fc2": by_layer([("L0_cond_W_fc2", "L0_cond_b_fc2"), ("L1_cond_w2", "L1_cond_b2")], plain),
        "marks": marks,
    }
    nc = bacc.Bacc("TRN2", target_bir_lowering=False, num_devices=1)
    aps = {k: nc.dram_tensor(f"in_{k}", a.shape, mb.dt.from_np(a.dtype), kind="ExternalInput").ap()
           for k, a in arrays.items()}
    out = nc.dram_tensor("out_x", x.shape, mb.dt.from_np(x.dtype), kind="ExternalOutput").ap()
    dit_two_blocks(nc, *aps.values(), out)
    r = run(nc, [{f"in_{k}": a for k, a in arrays.items()}], core_ids=[0])
    return r.results[0]["out_x"]
```
